# Optimizing a Trainium2 kernel written in Bass

```python
import numpy as np
import jax
import jax.numpy as jnp

def _softmax(x, axis=-1):
    return jax.nn.softmax(x, axis=axis)
def _gelu(x):
    return jax.nn.gelu(x, approximate=True)
def _silu(x):
    return jax.nn.silu(x)
def _sigmoid(x):
    return jax.nn.sigmoid(x)
def _layernorm(x, axis=-1, eps=1e-5):
    m = jnp.mean(x, axis=axis, keepdims=True)
    v = jnp.var(x, axis=axis, keepdims=True)
    return (x - m) / jnp.sqrt(v + eps)
def _scatter_add(tgt, idx, src, axis=0):
    return tgt.at[idx].add(src)
def _segment_sum(src, seg, n):
    return jax.ops.segment_sum(src, seg, n)

kernel_name = 'mk_vit_tower_cls_d1_tok_img256_59db6a'

def setup_inputs(seed: int = 0):
    np.random.seed(seed)
    _w = jnp.asarray
    def _rec_inputs():
        import jax
        import jax.numpy as jnp
        _rk = jax.random.key(seed)
        x = (-0.000222058 + 0.999998 * jax.random.normal(jax.random.fold_in(_rk, 1), (16, 3, 384, 384), jnp.float32))
        cls_tok = 0.02 * jax.random.normal(jax.random.fold_in(_rk, 5), (1, 1, 256), jnp.float32)
        return x, cls_tok
    x, cls_tok = _rec_inputs()
    def _L0_tok_setup():
        import jax, jax.numpy as jnp
        import numpy as np
        P = 16
        NUM_HEADS = 8
        WINDOW = 64

        def _layer_norm(x, w, b, eps=1e-05):
            mu = jnp.mean(x, axis=-1, keepdims=True)
            var = jnp.var(x, axis=-1, keepdims=True)
            return (x - mu) * jax.lax.rsqrt(var + eps) * w + b

        def _sinusoidal_pe(num_patches, num_features, dtype):
            pos = jnp.arange(num_patches, dtype=jnp.float32)[:, None]
            i = jnp.arange(0, num_features, 2, dtype=jnp.float32)
            div = jnp.exp(-jnp.log(10000.0) * i / num_features)
            ang = pos * div
            pe = jnp.stack([jnp.sin(ang), jnp.cos(ang)], axis=-1).reshape(num_patches, num_features)
            return pe.astype(dtype)

        def _ffn(x, w1, b1, w2, b2):
            h = jax.nn.gelu(jnp.einsum('bnd,hd->bnh', x, w1) + b1)
            return jnp.einsum('bnh,dh->bnd', h, w2) + b2

        def _windowed_attention(x, qkv_w, qkv_b, proj_w, proj_b):
            B, N, D = x.shape
            hd = D // NUM_HEADS
            qkv = jnp.einsum('bnd,ed->bne', x, qkv_w) + qkv_b
            qkv = qkv.reshape(B, N, 3, NUM_HEADS, hd)
            q, k, v = (qkv[:, :, 0], qkv[:, :, 1], qkv[:, :, 2])
            nw = N // WINDOW
            q = q.reshape(B, nw, WINDOW, NUM_HEADS, hd).transpose(0, 3, 1, 2, 4)
            k = k.reshape(B, nw, WINDOW, NUM_HEADS, hd).transpose(0, 3, 1, 2, 4)
            v = v.reshape(B, nw, WINDOW, NUM_HEADS, hd).transpose(0, 3, 1, 2, 4)
            scale = 1.0 / jnp.sqrt(jnp.asarray(hd, x.dtype))
            scores = jnp.einsum('bhwqd,bhwkd->bhwqk', q, k) * scale
            attn = jax.nn.softmax(scores, axis=-1)
            out = jnp.einsum('bhwqk,bhwkd->bhwqd', attn, v)
            out = out.transpose(0, 2, 3, 1, 4).reshape(B, N, D)
            return jnp.einsum('bnd,ed->bne', out, proj_w) + proj_b
        key = jax.random.key(seed)
        ks = jax.random.split(key, 8)
        D, HF = (256, 1024)
        s = lambda fan: 1.0 / np.sqrt(fan)
        return {'x': jax.random.normal(ks[0], (32, 3, 512, 512), jnp.float32), 'conv_w': jax.random.normal(ks[1], (D, 3, P, P), jnp.float32) * s(3 * P * P), 'conv_b': jnp.zeros((D,), jnp.float32), 'ln_w': jnp.ones((D,), jnp.float32), 'ln_b': jnp.zeros((D,), jnp.float32), 'qkv_w': jax.random.normal(ks[2], (3 * D, D), jnp.float32) * s(D), 'qkv_b': jnp.zeros((3 * D,), jnp.float32), 'proj_w': jax.random.normal(ks[3], (D, D), jnp.float32) * s(D), 'proj_b': jnp.zeros((D,), jnp.float32), 'ff_w1': jax.random.normal(ks[4], (HF, D), jnp.float32) * s(D), 'ff_b1': jnp.zeros((HF,), jnp.float32), 'ff_w2': jax.random.normal(ks[5], (D, HF), jnp.float32) * s(HF), 'ff_b2': jnp.zeros((D,), jnp.float32)}
    _L0_tok_all = _L0_tok_setup()
    _L0_tok_in = {k: v for k, v in _L0_tok_all.items() if k in ('conv_w', 'conv_b', 'ln_w', 'ln_b', 'qkv_w', 'qkv_b', 'proj_w', 'proj_b', 'ff_w1', 'ff_b1', 'ff_w2', 'ff_b2', )}
    del _L0_tok_all

    def _L0_attn_setup():
        import jax, jax.numpy as jnp
        import numpy as np
        B, S, DIN, DH = (8, 8192, 256, 256)

        def _log_g(x):
            return jnp.where(x >= 0, jnp.log(jax.nn.relu(x) + 0.5), -jax.nn.softplus(-x))

        def _mingru_layer(x, W, b):
            gh = jnp.einsum('bsd,ed->bse', x, W) + b
            gate, hidden = jnp.split(gh, 2, axis=-1)
            log_coeffs = -jax.nn.softplus(gate)
            log_vals = -jax.nn.softplus(-gate) + _log_g(hidden)
            Bb, Ss, Dd = log_coeffs.shape
            log_h0 = jnp.full((Bb, 1, Dd), jnp.log(0.5), log_coeffs.dtype)
            log_values = jnp.concatenate([log_h0, log_vals], axis=1)
            a_star = jnp.concatenate([jnp.zeros((Bb, 1, Dd), log_coeffs.dtype), jnp.cumsum(log_coeffs, axis=1)], axis=1)
            log_h = a_star + jax.lax.cumlogsumexp(log_values - a_star, axis=1)
            return jnp.exp(log_h)[:, 1:]

        def _reference_tuple_inner(x, W0, b0, W1, b1):
            out0 = _mingru_layer(x, W0, b0)
            out1 = _mingru_layer(out0, W1, b1)
            h = jnp.stack([out0[:, -1:], out1[:, -1:]])
            return (out1, h)
        key = jax.random.key(seed)
        k0, k1, k2, k3, k4 = jax.random.split(key, 5)
        stdv = 1.0 / np.sqrt(DIN)
        x = jax.random.normal(k0, (B, S, DIN), jnp.float32)
        W0 = jax.random.uniform(k1, (2 * DH, DIN), jnp.float32, -stdv, stdv)
        b0 = jax.random.uniform(k2, (2 * DH,), jnp.float32, -stdv, stdv)
        stdv2 = 1.0 / np.sqrt(DH)
        W1 = jax.random.uniform(k3, (2 * DH, DH), jnp.float32, -stdv2, stdv2)
        b1 = jax.random.uniform(k4, (2 * DH,), jnp.float32, -stdv2, stdv2)
        return {'x': x, 'W0': W0, 'b0': b0, 'W1': W1, 'b1': b1}
    _L0_attn_all = _L0_attn_setup()
    _L0_attn_in = {k: v for k, v in _L0_attn_all.items() if k in ('W0', 'b0', 'W1', 'b1', )}
    del _L0_attn_all

    def _L0_ffn_setup():
        import jax, jax.numpy as jnp
        import numpy as np
        E, D, H, TOP_K = (6, 256, 256, 2)
        ROUTER_H = D // 2
        key = jax.random.key(seed)
        ks = jax.random.split(key, 12)
        s = 1.0 / np.sqrt(D)
        sh = 1.0 / np.sqrt(H)
        sr = 1.0 / np.sqrt(ROUTER_H)
        return {'features': jax.random.normal(ks[0], (8, 4096, D), dtype=jnp.float32), 'router_w1': jax.random.uniform(ks[1], (D, ROUTER_H), jnp.float32, -s, s), 'router_b1': jnp.zeros((ROUTER_H,), jnp.float32), 'router_w2': jax.random.uniform(ks[2], (ROUTER_H, E), jnp.float32, -sr, sr), 'router_b2': jnp.zeros((E,), jnp.float32), 'expert_w1': jax.random.uniform(ks[3], (E, D, H), jnp.float32, -s, s), 'expert_b1': jnp.zeros((E, H), jnp.float32), 'expert_w2': jax.random.uniform(ks[4], (E, H, H), jnp.float32, -sh, sh), 'expert_b2': jnp.zeros((E, H), jnp.float32), 'expert_w3': jax.random.uniform(ks[5], (E, H, D), jnp.float32, -sh, sh), 'expert_b3': jnp.zeros((E, D), jnp.float32)}
    _L0_ffn_all = _L0_ffn_setup()
    _L0_ffn_in = {k: v for k, v in _L0_ffn_all.items() if k in ('router_w1', 'router_b1', 'router_w2', 'router_b2', 'expert_w1', 'expert_b1', 'expert_w2', 'expert_b2', 'expert_w3', 'expert_b3', )}
    del _L0_ffn_all

    return {
        "x": x,
        "cls_tok": cls_tok,
        "L0_tok_conv_w": _L0_tok_in["conv_w"],
        "L0_tok_conv_b": _L0_tok_in["conv_b"],
        "L0_tok_ln_w": _L0_tok_in["ln_w"],
        "L0_tok_ln_b": _L0_tok_in["ln_b"],
        "L0_tok_qkv_w": _L0_tok_in["qkv_w"],
        "L0_tok_qkv_b": _L0_tok_in["qkv_b"],
        "L0_tok_proj_w": _L0_tok_in["proj_w"],
        "L0_tok_proj_b": _L0_tok_in["proj_b"],
        "L0_tok_ff_w1": _L0_tok_in["ff_w1"],
        "L0_tok_ff_b1": _L0_tok_in["ff_b1"],
        "L0_tok_ff_w2": _L0_tok_in["ff_w2"],
        "L0_tok_ff_b2": _L0_tok_in["ff_b2"],
        "L0_attn_W0": _L0_attn_in["W0"],
        "L0_attn_b0": _L0_attn_in["b0"],
        "L0_attn_W1": _L0_attn_in["W1"],
        "L0_attn_b1": _L0_attn_in["b1"],
        "L0_ffn_router_w1": _L0_ffn_in["router_w1"],
        "L0_ffn_router_b1": _L0_ffn_in["router_b1"],
        "L0_ffn_router_w2": _L0_ffn_in["router_w2"],
        "L0_ffn_router_b2": _L0_ffn_in["router_b2"],
        "L0_ffn_expert_w1": _L0_ffn_in["expert_w1"],
        "L0_ffn_expert_b1": _L0_ffn_in["expert_b1"],
        "L0_ffn_expert_w2": _L0_ffn_in["expert_w2"],
        "L0_ffn_expert_b2": _L0_ffn_in["expert_b2"],
        "L0_ffn_expert_w3": _L0_ffn_in["expert_w3"],
        "L0_ffn_expert_b3": _L0_ffn_in["expert_b3"],
    }

def reference(x, cls_tok, L0_tok_conv_w, L0_tok_conv_b, L0_tok_ln_w, L0_tok_ln_b, L0_tok_qkv_w, L0_tok_qkv_b, L0_tok_proj_w, L0_tok_proj_b, L0_tok_ff_w1, L0_tok_ff_b1, L0_tok_ff_w2, L0_tok_ff_b2, L0_attn_W0, L0_attn_b0, L0_attn_W1, L0_attn_b1, L0_ffn_router_w1, L0_ffn_router_b1, L0_ffn_router_w2, L0_ffn_router_b2, L0_ffn_expert_w1, L0_ffn_expert_b1, L0_ffn_expert_w2, L0_ffn_expert_b2, L0_ffn_expert_w3, L0_ffn_expert_b3):
    import jax
    import jax.numpy as jnp
    def _L0_tok_ref(x, conv_w, conv_b, ln_w, ln_b, qkv_w, qkv_b, proj_w, proj_b, ff_w1, ff_b1, ff_w2, ff_b2):
        import jax, jax.numpy as jnp
        import numpy as np
        P = 16
        NUM_HEADS = 8
        WINDOW = 64

        def _layer_norm(x, w, b, eps=1e-05):
            mu = jnp.mean(x, axis=-1, keepdims=True)
            var = jnp.var(x, axis=-1, keepdims=True)
            return (x - mu) * jax.lax.rsqrt(var + eps) * w + b

        def _sinusoidal_pe(num_patches, num_features, dtype):
            pos = jnp.arange(num_patches, dtype=jnp.float32)[:, None]
            i = jnp.arange(0, num_features, 2, dtype=jnp.float32)
            div = jnp.exp(-jnp.log(10000.0) * i / num_features)
            ang = pos * div
            pe = jnp.stack([jnp.sin(ang), jnp.cos(ang)], axis=-1).reshape(num_patches, num_features)
            return pe.astype(dtype)

        def _ffn(x, w1, b1, w2, b2):
            h = jax.nn.gelu(jnp.einsum('bnd,hd->bnh', x, w1) + b1)
            return jnp.einsum('bnh,dh->bnd', h, w2) + b2

        def _windowed_attention(x, qkv_w, qkv_b, proj_w, proj_b):
            B, N, D = x.shape
            hd = D // NUM_HEADS
            qkv = jnp.einsum('bnd,ed->bne', x, qkv_w) + qkv_b
            qkv = qkv.reshape(B, N, 3, NUM_HEADS, hd)
            q, k, v = (qkv[:, :, 0], qkv[:, :, 1], qkv[:, :, 2])
            nw = N // WINDOW
            q = q.reshape(B, nw, WINDOW, NUM_HEADS, hd).transpose(0, 3, 1, 2, 4)
            k = k.reshape(B, nw, WINDOW, NUM_HEADS, hd).transpose(0, 3, 1, 2, 4)
            v = v.reshape(B, nw, WINDOW, NUM_HEADS, hd).transpose(0, 3, 1, 2, 4)
            scale = 1.0 / jnp.sqrt(jnp.asarray(hd, x.dtype))
            scores = jnp.einsum('bhwqd,bhwkd->bhwqk', q, k) * scale
            attn = jax.nn.softmax(scores, axis=-1)
            out = jnp.einsum('bhwqk,bhwkd->bhwqd', attn, v)
            out = out.transpose(0, 2, 3, 1, 4).reshape(B, N, D)
            return jnp.einsum('bnd,ed->bne', out, proj_w) + proj_b
        B, C, H, W = x.shape
        D = conv_w.shape[0]
        nH, nW = (H // P, W // P)
        patches = x.reshape(B, C, nH, P, nW, P).transpose(0, 2, 4, 1, 3, 5).reshape(B, nH * nW, C * P * P)
        h = jnp.einsum('bnp,dp->bnd', patches, conv_w.reshape(D, -1)) + conv_b
        h = _layer_norm(h, ln_w, ln_b)
        h = h + _sinusoidal_pe(h.shape[1], D, h.dtype)
        identity = h
        h = _ffn(h, ff_w1, ff_b1, ff_w2, ff_b2)
        h = _windowed_attention(h, qkv_w, qkv_b, proj_w, proj_b)
        h = h + identity
        identity = h
        h = _ffn(h, ff_w1, ff_b1, ff_w2, ff_b2)
        return h + identity

    def _L0_attn_ref(x, W0, b0, W1, b1):
        import jax, jax.numpy as jnp
        import numpy as np
        B, S, DIN, DH = (8, 8192, 256, 256)

        def _log_g(x):
            return jnp.where(x >= 0, jnp.log(jax.nn.relu(x) + 0.5), -jax.nn.softplus(-x))

        def _mingru_layer(x, W, b):
            gh = jnp.einsum('bsd,ed->bse', x, W) + b
            gate, hidden = jnp.split(gh, 2, axis=-1)
            log_coeffs = -jax.nn.softplus(gate)
            log_vals = -jax.nn.softplus(-gate) + _log_g(hidden)
            Bb, Ss, Dd = log_coeffs.shape
            log_h0 = jnp.full((Bb, 1, Dd), jnp.log(0.5), log_coeffs.dtype)
            log_values = jnp.concatenate([log_h0, log_vals], axis=1)
            a_star = jnp.concatenate([jnp.zeros((Bb, 1, Dd), log_coeffs.dtype), jnp.cumsum(log_coeffs, axis=1)], axis=1)
            log_h = a_star + jax.lax.cumlogsumexp(log_values - a_star, axis=1)
            return jnp.exp(log_h)[:, 1:]

        def _reference_tuple_inner(x, W0, b0, W1, b1):
            out0 = _mingru_layer(x, W0, b0)
            out1 = _mingru_layer(out0, W1, b1)
            h = jnp.stack([out0[:, -1:], out1[:, -1:]])
            return (out1, h)
        return _reference_tuple_inner(x, W0, b0, W1, b1)[0]

    def _L0_ffn_ref(features, router_w1, router_b1, router_w2, router_b2, expert_w1, expert_b1, expert_w2, expert_b2, expert_w3, expert_b3):
        import jax, jax.numpy as jnp
        import numpy as np
        E, D, H, TOP_K = (6, 256, 256, 2)
        ROUTER_H = D // 2
        rh = jax.nn.relu(features @ router_w1 + router_b1)
        expert_logits = jax.nn.softmax(rh @ router_w2 + router_b2, axis=-1)
        top_w, top_i = jax.lax.top_k(expert_logits, TOP_K)
        routing_weights = jax.nn.softmax(top_w, axis=-1)
        h1 = jax.nn.relu(jnp.einsum('bsd,edh->bseh', features, expert_w1) + expert_b1)
        h2 = jax.nn.relu(jnp.einsum('bseh,ehf->bsef', h1, expert_w2) + expert_b2)
        expert_out = jnp.einsum('bsef,efo->bseo', h2, expert_w3) + expert_b3
        sel = jnp.take_along_axis(expert_out, top_i[:, :, :, None], axis=2)
        combined = jnp.sum(sel * routing_weights[..., None], axis=2)
        return combined

    h = _L0_tok_ref(x, L0_tok_conv_w, L0_tok_conv_b, L0_tok_ln_w, L0_tok_ln_b, L0_tok_qkv_w, L0_tok_qkv_b, L0_tok_proj_w, L0_tok_proj_b, L0_tok_ff_w1, L0_tok_ff_b1, L0_tok_ff_w2, L0_tok_ff_b2)
    h = jnp.concatenate([jnp.broadcast_to(cls_tok, (h.shape[0], 1, h.shape[2])), h], axis=1)
    h = h + _L0_attn_ref(_layernorm(h, axis=-1), L0_attn_W0, L0_attn_b0, L0_attn_W1, L0_attn_b1)
    h = h + _L0_ffn_ref(_layernorm(h, axis=-1), L0_ffn_router_w1, L0_ffn_router_b1, L0_ffn_router_w2, L0_ffn_router_b2, L0_ffn_expert_w1, L0_ffn_expert_b1, L0_ffn_expert_w2, L0_ffn_expert_b2, L0_ffn_expert_w3, L0_ffn_expert_b3)
    return h


_drawn_inputs = setup_inputs


def setup_inputs(seed=0):
    import zlib

    import numpy as np

    out = dict(_drawn_inputs(seed))
    spreads = {'L0_tok_conv_b': (0.0, 0.1),
     'L0_tok_ln_w': (1.0, 0.2),
     'L0_tok_ln_b': (0.0, 0.1),
     'L0_tok_qkv_b': (0.0, 0.1),
     'L0_tok_proj_b': (0.0, 0.1),
     'L0_tok_ff_b1': (0.0, 0.1),
     'L0_tok_ff_b2': (0.0, 0.1),
     'L0_ffn_router_b1': (0.0, 0.384),
     'L0_ffn_router_b2': (0.0, 0.1),
     'L0_ffn_expert_b1': (0.0, 0.8),
     'L0_ffn_expert_b2': (0.0, 0.546),
     'L0_ffn_expert_b3': (0.0, 0.1)}
    factors = {'cls_tok': 64.0, 'L0_attn_b0': 8.0, 'L0_attn_b1': 4.106}
    for name, (base, spread) in spreads.items():
        noise = np.random.default_rng([zlib.crc32(name.encode()), seed]).standard_normal(out[name].shape)
        drawn = base * np.exp(spread * noise) if base else spread * noise
        out[name] = jnp.asarray(drawn.astype(out[name].dtype))
    for name, factor in factors.items():
        out[name] = (out[name] * factor).astype(out[name].dtype)
    return out
```

```python
from contextlib import ExitStack

import numpy as np

import concourse.bass as bass
from concourse import mybir

ALU = mybir.AluOpType
ACT = mybir.ActivationFunctionType
AX_X = mybir.AxisListType.X
F32 = mybir.dt.float32
F16 = mybir.dt.float16
U32 = mybir.dt.uint32

P = 128
IMAGES, CHANNELS, SIDE, PATCH = 16, 3, 384, 16
D = 256
M = D // P
PATCHES = (SIDE // PATCH) ** 2
TOKENS = IMAGES * PATCHES
SEQ = PATCHES + 1
KP = CHANNELS * PATCH * PATCH // P
HF = 1024
MH = HF // P
HEADS, WINDOW = 8, 64
HD = D // HEADS
EXPERTS = 6
ROUTER = D // 2

N = 384
CH = 2
STEPS = TOKENS // (N * CH)
PAIRS = N // (2 * WINDOW)
WINDOWS = N // WINDOW
VALUES = 2
VROWS = WINDOWS // VALUES * 4
POSITIONS = 3
assert (N * POSITIONS) % PATCHES == 0

HALF = [SEQ - SEQ // 2, SEQ // 2]
START = [0, HALF[0]]
TILES = 3
TILE = [HALF[0] // TILES + 1, HALF[1] // TILES]
TSTEP = HALF[1] // TILES

WS = 64.0
INV = 1.0 / WS
EPS = 1e-5

def _columns(sizes):
    at, out = 0, {}
    for name, size in sizes:
        out[name] = at
        at += size
    return out, at


WA, WA_COLS = _columns([("conv", KP * D), ("ff1", M * HF), ("ff2", MH * D), ("qkv", M * 3 * D), ("proj", M * D)])
WB, WB_COLS = _columns([("gru0", M * 2 * D), ("gru1", M * 2 * D), ("router1", M * ROUTER),
                        ("expert1", EXPERTS * M * D), ("expert2", EXPERTS * M * D), ("expert3", EXPERTS * M * D)])
BC, BC_COLS = _columns([("conv", M), ("ln_w", M), ("ln_b", M), ("ff1", MH), ("ff2", M), ("qkv", 3 * M), ("proj", M),
                        ("gru0", 2 * M), ("gru1", 2 * M), ("router1", 1), ("expert1", EXPERTS * M),
                        ("expert2", EXPERTS * M), ("router2", EXPERTS), ("router2_w", EXPERTS), ("cls", M)])
WA_PARTS = [(0, KP * D), (WA["ff1"], M * HF), (WA["ff2"], MH * D), (WA["qkv"], M * 3 * D), (WA["proj"], M * D)]
WB_PART = WB_COLS // 15


def bank_plan(order, banks):
    uses, place = {b: 0 for b in banks}, {}
    for n, group in enumerate(order):
        b = banks[n % len(banks)]
        place[group] = (b, uses[b])
        uses[b] += 1
    return place, uses


TOKENIZER = [
    ("conv", 0), ("conv", 1), ("mean", 0), ("mean", 1), ("var", 0), ("var", 1),
    ("up0", 0), ("up0", 1), ("down0", 0), ("down0", 1), ("patches", 0), ("patches", 1),
    ("query_key", 0), ("value", 0), ("score", 0), ("query_key", 1), ("value", 1), ("score", 1),
    ("turn", 0), ("mix", 0), ("turn", 1), ("mix", 1), ("proj", 0), ("proj", 1),
    ("up1", 0), ("up1", 1), ("down1", 0), ("down1", 1),
]
GROUPS = {"conv": M, "mean": 1, "var": 1, "up0": MH, "up1": MH, "down0": M, "down1": M, "query_key": 2 * M,
          "value": VALUES, "score": PAIRS, "turn": PAIRS, "mix": PAIRS, "proj": M, "patches": 0}

LAYER = [
    ("mean1", 0), ("mean1", 1), ("var1", 0), ("var1", 1), ("gru0", 0), ("gru0", 1), ("gru1", 0), ("gru1", 1),
    ("mean2", 0), ("mean2", 1), ("var2", 0), ("var2", 1), ("route", 0), ("route", 1),
    ("share", 0), ("experts", 0), ("share", 1), ("experts", 1),
]
LAG2, LAG3 = 1, 3


def tokenizer_groups():
    return [(s, c, n) for s, c in TOKENIZER for n in range(GROUPS[s])]


def expert_steps():
    for s in range(EXPERTS + LAG3):
        if s < EXPERTS:
            yield 1, s
        if 0 <= s - LAG2 < EXPERTS:
            yield 2, s - LAG2
        if 0 <= s - LAG3 < EXPERTS:
            yield 3, s - LAG3


def layer_groups():
    o = []
    for s, c in LAYER:
        if s == "experts":
            o += [("expert%d" % k, c, e * M + m) for k, e in expert_steps() if k < 3 for m in range(M)]
        elif s == "route":
            o += [(x, c, 0) for x in ("router1", "router2", "weights")]
        else:
            n = EXPERTS if s == "share" else 2 * M if s in ("gru0", "gru1") else 1
            o += [(s, c, k) for k in range(n)]
    return o



TOKENIZER_SIGNALS = {
    "raw_hi": 1, "raw_lo": 1, "conv_out": M, "mean_out": 1, "squared": 1, "var_out": 1, "inverse": 1, "normed": 1,
    "affine": M, "residual": 1, "x0_hi": 1, "x0_lo": 1, "up0_out": MH, "up0_hi": MH, "up0_lo": MH, "down0_out": M,
    "down0_hi": M, "down0_lo": M, "query_key_out": 2 * M, "q_hi": M, "q_lo": M, "k_lo": M, "v_hi": VALUES,
    "value_out": VALUES, "score_top": PAIRS, "score_out": PAIRS, "prob_exp": PAIRS, "prob_sum": PAIRS,
    "prob_rec": PAIRS, "prob_out": PAIRS, "turn_hi": PAIRS, "turn_out": PAIRS, "mix_out": PAIRS, "mix_hi": PAIRS,
    "mix_lo": PAIRS, "proj_out": M, "attended": M, "x1_hi": M, "x1_lo": M, "up1_out": MH, "up1_hi": MH,
    "up1_lo": MH, "down1_out": M, "tokens_out": M,
}
FULL_USERS = {"up0": (MH, "up0_lo"), "up1": (MH, "up1_lo"), "down0": (M, "down0_lo"), "mix": (PAIRS, "mix_lo"),
              "proj": (M, "attended"), "down1": (M, "tokens_out")}
RING = 2

ROUTE_STEPS = 19
LAYER_SIGNALS = {
    "mean1_out": 1, "squared1": 1, "var1_out": 1, "inverse1": 1, "normed1": 1, "norm1_hi": 1, "norm1_lo": 1,
    "gru0_out": 2 * M, "gru1_out": 2 * M, "candidate0": M, "candidate1": M, "taken0": M, "taken1": M,
    "state0": M, "state1": M, "state0_hi": 1, "state0_lo": 1, "mixed": 1,
    "mean2_out": 1, "squared2": 1, "var2_out": 1, "inverse2": 1, "normed2": 1, "norm2_hi": 1, "norm2_lo": 1,
    "router1_out": 1, "router2_out": 1, "route": ROUTE_STEPS, "router_exp": 1, "router_exp2": 1, "weights_out": 1,
    "share_out": EXPERTS, "expert1_out": EXPERTS * M, "h1_hi": EXPERTS * M, "h1_lo": EXPERTS * M,
    "expert2_out": EXPERTS * M, "h2_weighted": EXPERTS * M, "h2_hi": EXPERTS * M, "h2_lo": EXPERTS * M,
    "sums_full": M, "combined": M,
}
RING1, RING2 = 2, 3


def full_order():
    o = []
    for s, c in TOKENIZER:
        if s == "query_key":
            o += [((s, c, n), "q_lo" if n < M else "k_lo", n % M) for n in range(2 * M)]
        elif s in FULL_USERS:
            n, name = FULL_USERS[s]
            o += [((s, c, k), name, k) for k in range(n)]
    return o


def build_program(nc, patches, pos, wa, wb, cols, b3, ident, out, images=IMAGES):
    steps = images * PATCHES // (N * CH)
    tok = nc.dram_tensor("tokens_dram", (P, M, TOKENS), F32, kind="Internal").ap()

    with ExitStack() as whole:
        def sb(ctx, name, shape, dt=F32):
            return ctx.enter_context(nc.sbuf_tensor(name, shape, dt))

        def sem(name):
            return whole.enter_context(nc.semaphore(name))

        wah = sb(whole, "wah", [P, WA_COLS], F16)
        wal = sb(whole, "wal", [P, WA_COLS], F16)
        wbh = sb(whole, "wbh", [P, WB_COLS], F16)
        wbl = sb(whole, "wbl", [P, WB_COLS], F16)
        col = sb(whole, "col", [P, BC_COLS])
        ncol = sb(whole, "ncol", [P, BC_COLS])
        epsc = sb(whole, "epsc", [P, 1])
        scale = sb(whole, "scale", [P, 1])
        ones = sb(whole, "ones", [P, P])
        idf = sb(whole, "idf", [P, P])
        idh = sb(whole, "idh", [P, P], F16)
        b3raw = sb(whole, "b3raw", [2 * EXPERTS, D + EXPERTS * P])
        b3h = sb(whole, "b3h", [2 * EXPERTS, D], F16)
        b3l = sb(whole, "b3l", [2 * EXPERTS, D], F16)
        sel = sb(whole, "sel", [2 * EXPERTS, EXPERTS * P], F16)
        wbraw = sb(whole, "wbraw", [P, WB_PART])
        bank = [whole.enter_context(nc.psum_tensor("bank%d" % b, [P, 512], F32)) for b in range(8)]

        consts_loaded, consts_made = sem("consts_loaded"), sem("consts_made")
        wa_loaded = [sem("wa_loaded%d" % n) for n in range(len(WA_PARTS))]
        wa_hi, wa_lo = sem("wa_hi"), sem("wa_lo")
        wb_loaded, wb_scaled, wb_hi, wb_lo = (sem("wb_" + s) for s in ("loaded", "scaled", "hi", "lo"))
        bank_full = [sem("bank_full%d" % b) for b in range(8)]
        raw_loaded = [sem("raw_loaded%d" % c) for c in range(CH)]
        tokens_stored = [sem("tokens_stored%d" % c) for c in range(CH)]
        S = {n: sem(n) for n in TOKENIZER_SIGNALS}
        tokens_loaded = sem("tokens_loaded")
        out_stored = [sem("out_stored%d" % c) for c in range(CH)]
        L = {n: sem(n) for n in LAYER_SIGNALS}

        def count(signals, name, t, n=0):
            return signals[name] * (t + CH) + n + 1

        def weight(block, base, k, width, a, b):
            return block[:, base + k * width + a:base + k * width + b]

        def bias(table, name, m, a=0, b=P):
            return table[a:b, BC[name] + m:BC[name] + m + 1]

        def product(pe, o, terms):
            for k, ((wh, wl), (xh, xl)) in enumerate(terms):
                pe.matmul(o, wh, xh, start=(k == 0), stop=False)
                pe.matmul(o, wh, xl, start=False, stop=False)
                mm = pe.matmul(o, wl, xh, start=False, stop=(k == len(terms) - 1))
            return mm

        placeA, usesA = bank_plan(tokenizer_groups(), list(range(8)))
        placeB, usesB = bank_plan(layer_groups(), list(range(6)))
        fulls = full_order()
        assert len(fulls) % RING == 0
        full_at = {key: n for n, (key, _, _) in enumerate(fulls)}

        with ExitStack() as ctx:
            raw = sb(ctx, "raw", [P, CH, KP * N])
            table = sb(ctx, "table", [P, CH, M * N])
            pat_h = sb(ctx, "pat_h", [P, CH, KP * N], F16)
            pat_l = sb(ctx, "pat_l", [P, CH, KP * N], F16)
            z = sb(ctx, "z", [P, CH, M, N])
            res = sb(ctx, "res", [P, CH, M, N])
            vexp_h = sb(ctx, "vexp_h", [P, CH, WINDOWS * 4, 2 * HD], F16)
            vexp_l = sb(ctx, "vexp_l", [P, CH, WINDOWS * 4, 2 * HD], F16)
            kexp_h = sb(ctx, "kexp_h", [P, M, WINDOWS, 4, WINDOW], F16)
            kexp_l = sb(ctx, "kexp_l", [P, M, WINDOWS, 4, WINDOW], F16)

            with ExitStack() as first:
                wraw = sb(first, "wraw", [P, 2, M * HF])
                block = first.enter_context(nc.Block())

                @block.sync
                def _(sp):
                    sp.dma_start(wraw[:, 0, 0:WA_PARTS[0][1]], wa[:, 0:WA_PARTS[0][1]]).then_inc(wa_loaded[0], 16)
                    for c in range(CH):
                        sp.dma_start(raw[:, c, :], patches[c]).then_inc(raw_loaded[c], 16)
                        sp.dma_start(table[:, c, :], pos[c]).then_inc(raw_loaded[c], 16)
                    for src, dst in ((cols, col[:, :]), (ident, idf[:, :]), (b3, b3raw[:, :])):
                        sp.dma_start(dst, src).then_inc(consts_loaded, 16)
                    for n, (a, size) in enumerate(WA_PARTS):
                        if n == 0:
                            continue
                        if n >= 2:
                            sp.wait_ge(wa_lo, n - 1)
                        sp.dma_start(wraw[:, n % 2, 0:size], wa[:, a:a + size]).then_inc(wa_loaded[n], 16)

                @block.scalar
                def _(act):
                    for n, (a, size) in enumerate(WA_PARTS):
                        act.wait_ge(wa_loaded[n], 16)
                        act.activation(wah[:, a:a + size], wraw[:, n % 2, 0:size], ACT.Copy, scale=WS).then_inc(wa_hi, 1)
                        if n == 0:
                            for c in range(CH):
                                act.wait_ge(raw_loaded[c], 32)
                                act.activation(pat_h[:, c, :], raw[:, c, :], ACT.Copy).then_inc(S["raw_hi"], 1)

                @block.vector
                def _(dve):
                    for name, per in TOKENIZER_SIGNALS.items():
                        dve.sem_inc(S[name], per * CH)
                    for name, per in LAYER_SIGNALS.items():
                        dve.sem_inc(L[name], per * CH)
                    for c in range(CH):
                        dve.sem_inc(tokens_stored[c], 16)
                        dve.sem_inc(out_stored[c], 16)
                    for n, (a, size) in enumerate(WA_PARTS):
                        dve.wait_ge(wa_hi, n + 1)
                        dve.scalar_tensor_tensor(wal[:, a:a + size], wraw[:, n % 2, 0:size], WS, wah[:, a:a + size],
                                                 ALU.mult, ALU.subtract).then_inc(wa_lo, 1)
                        if n == 0:
                            for c in range(CH):
                                dve.wait_ge(S["raw_hi"], count(TOKENIZER_SIGNALS, "raw_hi", c))
                                dve.tensor_tensor(pat_l[:, c, :], raw[:, c, :], pat_h[:, c, :], ALU.subtract).then_inc(S["raw_lo"], 1)

                @block.gpsimd
                def _(pool):
                    pool.memset(ones[:, :], 1.0 / D).then_inc(consts_made, 1)
                    pool.memset(epsc[:, :], EPS).then_inc(consts_made, 1)
                    pool.memset(scale[:, :], WS).then_inc(consts_made, 1)
                    for t in (kexp_h, kexp_l, vexp_h, vexp_l):
                        pool.memset(t[:], 0.0).then_inc(consts_made, 1)
                    pool.wait_ge(consts_loaded, 48)
                    pool.tensor_scalar(ncol[:, :], col[:, :], -1.0, None, ALU.mult).then_inc(consts_made, 1)
                    pool.tensor_copy(idh[:, :], idf[:, :]).then_inc(consts_made, 1)
                    pool.tensor_copy(sel[:, :], b3raw[:, D:D + EXPERTS * P]).then_inc(consts_made, 1)
                    pool.tensor_scalar(b3raw[:, 0:D], b3raw[:, 0:D], WS, None, ALU.mult).then_inc(consts_made, 1)
                    pool.wait_ge(consts_made, 11)
                    pool.tensor_copy(b3h[:, :], b3raw[:, 0:D]).then_inc(consts_made, 1)
                    pool.wait_ge(consts_made, 12)
                    pool.tensor_tensor(b3l[:, :], b3raw[:, 0:D], b3h[:, :], ALU.subtract).then_inc(consts_made, 1)

            with ExitStack() as second:
                hid_h = sb(second, "hid_h", [P, CH, MH, N], F16)
                hid_l = sb(second, "hid_l", [P, CH, MH, N], F16)
                x_h = sb(second, "x_h", [P, CH, M, N], F16)
                x_l = sb(second, "x_l", [P, CH, M, N], F16)
                std = sb(second, "std", [P, CH, N])
                full = sb(second, "full", [P, RING, N])
                q_h, q_l = hid_l[:, :, 0:M, :], hid_l[:, :, M:2 * M, :]
                prob = hid_h[:, :, :, :].rearrange("p c m n -> p (c m n)").bitcast(F32).rearrange(
                    "p (c a h k) -> p c a h k", c=CH, a=PAIRS, h=HEADS)
                pt_h = sb(second, "pt_h", [P, PAIRS, 4, P], F16)
                pt_l = sb(second, "pt_l", [P, PAIRS, 4, P], F16)
                top = sb(second, "top", [P, CH, PAIRS, HEADS])
                rec = sb(second, "rec", [P, CH, PAIRS, HEADS])
                block = second.enter_context(nc.Block())

                def at(name, t, n=0):
                    return count(TOKENIZER_SIGNALS, name, t, n)

                def product_of(eng, i, key):
                    b, k = placeA[key]
                    eng.wait_ge(bank_full[b], i * usesA[b] + k + 1)
                    return bank[b]

                @block.sync
                def _(sp):
                    def load(step, c, t):
                        sp.wait_ge(S["raw_lo"], at("raw_lo", t))
                        sp.dma_start(raw[:, c, :], patches[bass.ds(step, 1)].rearrange("a p n -> (a p) n")
                                     ).then_inc(raw_loaded[c], 16)
                        sp.wait_ge(S["residual"], at("residual", t))
                        sp.dma_start(table[:, c, :], pos[bass.ds(step, 1)].rearrange("a p n -> (a p) n")
                                     ).then_inc(raw_loaded[c], 16)

                    def store(t, c):
                        sp.wait_ge(S["tokens_out"], at("tokens_out", t, M - 1))
                        sp.dma_start(tok[:, :, bass.ds(t * N, N)], z[:, c, :, :]).then_inc(tokens_stored[c], 16)

                    with sp.Fori(0, steps - 1) as i:
                        for c in range(CH):
                            load(CH * i + CH + c, c, CH * i + c)
                        for c in range(CH):
                            store(CH * i + c, c)
                    for c in range(CH):
                        load(c, c, CH * (steps - 1) + c)
                    for c in range(CH):
                        store(CH * (steps - 1) + c, c)
                    for c in range(CH):
                        sp.wait_ge(tokens_stored[c], 16 * steps + 16)

                @block.gpsimd
                def _(pool):
                    with pool.Fori(0, WB_COLS // WB_PART) as n:
                        cut = bass.ds(n * WB_PART, WB_PART)
                        pool.dma_start(wbraw[:, :], wb[:, cut]).then_inc(wb_loaded, 16)
                        pool.wait_ge(wb_loaded, 16 * n + 16)
                        pool.tensor_tensor(wbraw[:, :], wbraw[:, :], scale[:, 0:1].broadcast_to([P, WB_PART]),
                                           ALU.mult).then_inc(wb_scaled, 1)
                        pool.wait_ge(wb_scaled, n + 1)
                        pool.tensor_copy(wbh[:, cut], wbraw[:, :]).then_inc(wb_hi, 1)
                        pool.wait_ge(wb_hi, n + 1)
                        pool.tensor_tensor(wbl[:, cut], wbraw[:, :], wbh[:, cut], ALU.subtract).then_inc(wb_lo, 1)
                        pool.wait_ge(wb_lo, n + 1)

                @block.tensor
                def _(pe):
                    groups = tokenizer_groups()
                    with pe.Fori(0, steps) as i:
                        def group(key, ready=None):
                            b, k = placeA[key]
                            n = groups.index(key)
                            s, c, m = groups[n - 8] if n >= 8 else groups[[g for g in range(len(groups)) if placeA[groups[g]][0] == b][-1]]
                            t = CH * i + c - (0 if n >= 8 else CH)
                            if ready is not None:
                                pe.wait_ge(S[ready[0]], at(*ready))
                            if ready is None or ready[0] != s + "_out":
                                pe.wait_ge(S[s + "_out"], at(s + "_out", t, m))
                            return bank[b], bank_full[b]

                        def linear(stage, c, ready, name, mtiles, ktiles, width, xh, xl):
                            for m in range(mtiles):
                                o, filled = group((stage, c, m), ready if m == 0 else None)
                                product(pe, o[:, 0:N], [
                                    ([weight(w, WA[name], k, width, m * P, m * P + P) for w in (wah, wal)], (xh(k), xl(k)))
                                    for k in range(ktiles)]).then_inc(filled, 1)

                        for stage, c in TOKENIZER:
                            t = CH * i + c
                            xs = (lambda k, c=c: x_h[:, c, k, :]), (lambda k, c=c: x_l[:, c, k, :])
                            if stage == "conv":
                                linear(stage, c, ("raw_lo", t), "conv", M, KP, D, lambda k: pat_h[:, c, k * N:(k + 1) * N],
                                       lambda k: pat_l[:, c, k * N:(k + 1) * N])
                            elif stage in ("mean", "var"):
                                src, ready = (z, ("conv_out", t, M - 1)) if stage == "mean" else (res, ("squared", t))
                                o, filled = group((stage, c, 0), ready)
                                for m in range(M):
                                    mm = pe.matmul(o[:, 0:N], ones[:, :], src[:, c, m, :], start=(m == 0), stop=(m == M - 1))
                                mm.then_inc(filled, 1)
                            elif stage in ("up0", "up1"):
                                ready = ("x0_lo", t) if stage == "up0" else ("x1_lo", t, M - 1)
                                linear(stage, c, ready, "ff1", MH, M, HF, *xs)
                            elif stage in ("down0", "down1"):
                                ready = ("up0_lo" if stage == "down0" else "up1_lo", t, MH - 1)
                                linear(stage, c, ready, "ff2", M, MH, D, lambda k: hid_h[:, c, k, :], lambda k: hid_l[:, c, k, :])
                            elif stage == "query_key":
                                linear(stage, c, ("down0_lo", t, M - 1), "qkv", 2 * M, M, 3 * D, *xs)
                            elif stage == "value":
                                for n in range(VALUES):
                                    o, filled = group((stage, c, n))
                                    for w in range(WINDOWS // VALUES):
                                        a = (n * (WINDOWS // VALUES) + w) * WINDOW
                                        for r in range(2):
                                            mm = product(pe, o[r * 64:r * 64 + 64, w * P:w * P + P], [
                                                ([x[:, c, k, a:a + WINDOW] for x in (x_h, x_l)],
                                                 [weight(x, WA["qkv"], k, 3 * D, 2 * D, 3 * D).rearrange("p (g x) -> p g x", g=4)[:, :, r * HD:r * HD + HD]
                                                  for x in (wah, wal)])
                                                for k in range(M)])
                                    mm.then_inc(filled, 1)
                            elif stage == "score":
                                pe.wait_ge(S["q_lo"], at("q_lo", t, M - 1))
                                pe.wait_ge(S["k_lo"], at("k_lo", t, M - 1))
                                for p in range(PAIRS):
                                    o, filled = group((stage, c, p))
                                    for w in range(2):
                                        a = (2 * p + w) * WINDOW
                                        for f in range(M):
                                            mm = product(pe, o[w * WINDOW:(w + 1) * WINDOW, f * 256:(f + 1) * 256], [
                                                ([x[:, c, f, a:a + WINDOW] for x in (q_h, q_l)],
                                                 [x[:, f, 2 * p + w, :, :].rearrange("p a b -> p (a b)") for x in (kexp_h, kexp_l)])])
                                    mm.then_inc(filled, 1)
                            elif stage == "turn":
                                for p in range(PAIRS):
                                    o, filled = group((stage, c, p), ("prob_out", t, p))
                                    for h in range(4):
                                        mm = pe.transpose(o[:, h * P:(h + 1) * P],
                                                          prob[:, c, p, 2 * h:2 * h + 2, :].rearrange("p a b -> p (a b)"), idf[:, :])
                                    mm.then_inc(filled, 1)
                            elif stage == "mix":
                                for p in range(PAIRS):
                                    o, filled = group((stage, c, p), ("turn_out", t, p))
                                    for h in range(4):
                                        for w in range(2):
                                            r = (h % 2) * 2 * HD
                                            a = (h // 2) * P + w * WINDOW
                                            mm = product(pe, o[r:r + 2 * HD, a:a + WINDOW], [
                                                ([x[:, c, (2 * p + w) * 4 + h, :] for x in (vexp_h, vexp_l)],
                                                 [x[:, p, h, w * WINDOW:(w + 1) * WINDOW] for x in (pt_h, pt_l)])])
                                    mm.then_inc(filled, 1)
                            elif stage == "proj":
                                linear(stage, c, ("mix_lo", t, PAIRS - 1), "proj", M, M, D, *xs)

                @block.scalar
                def _(act):
                    act.wait_ge(consts_made, 13)
                    with act.Fori(0, steps) as i:
                        def keep(key):
                            n = full_at[key]
                            (s, c, _), name, k = fulls[n - RING]
                            act.wait_ge(S[name], at(name, CH * i + c - (0 if n >= RING else CH), k))
                            return full[:, n % RING, :]

                        for stage, c in TOKENIZER:
                            t = CH * i + c
                            if stage == "conv":
                                act.wait_ge(tokens_stored[c], 16 * i + 16)
                                for m in range(M):
                                    o = product_of(act, i, (stage, c, m))
                                    act.activation(z[:, c, m, :], o[:, 0:N], ACT.Identity, bias=bias(col, "conv", m),
                                                   scale=INV).then_inc(S["conv_out"], 1)
                            elif stage == "patches":
                                act.wait_ge(raw_loaded[c], 32 * i + 64)
                                act.activation(pat_h[:, c, :], raw[:, c, :], ACT.Copy).then_inc(S["raw_hi"], 1)
                            elif stage == "mean":
                                act.wait_ge(S["mean_out"], at("mean_out", t))
                                act.activation(res[:, c, :, :], z[:, c, :, :], ACT.Square).then_inc(S["squared"], 1)
                            elif stage == "var":
                                o = product_of(act, i, (stage, c, 0))
                                act.activation(std[:, c, :], o[:, 0:N], ACT.Sqrt, bias=epsc[:, 0:1]).then_inc(S["var_out"], 1)
                                act.wait_ge(S["normed"], at("normed", t))
                                for m in range(M):
                                    act.activation(res[:, c, m, :], z[:, c, m, :], ACT.Identity, bias=bias(col, "ln_b", m),
                                                   scale=bias(col, "ln_w", m)).then_inc(S["affine"], 1)
                            elif stage in ("up0", "up1"):
                                for m in range(MH):
                                    f = keep((stage, c, m))
                                    o = product_of(act, i, (stage, c, m))
                                    act.activation(f, o[:, 0:N], ACT.Gelu_apprx_tanh, bias=bias(col, "ff1", m),
                                                   scale=INV).then_inc(S[stage + "_out"], 1)
                            elif stage in ("down0", "down1", "proj"):
                                for m in range(M):
                                    f = keep((stage, c, m))
                                    o = product_of(act, i, (stage, c, m))
                                    act.activation(f, o[:, 0:N], ACT.Identity, bias=bias(col, "proj" if stage == "proj" else "ff2", m),
                                                   scale=INV).then_inc(S[stage + "_out"], 1)
                            elif stage == "query_key":
                                for n in range(2 * M):
                                    f = keep((stage, c, n))
                                    o = product_of(act, i, (stage, c, n))
                                    a = act.activation(f, o[:, 0:N], ACT.Identity, bias=bias(col, "qkv", n), scale=INV)
                                    if n >= M:
                                        for h in range(4):
                                            r, e = h * HD, h * HD + HD
                                            a = act.activation(kexp_h[r:e, n - M, :, h, :],
                                                               o[r:e, 0:N].rearrange("p (w k) -> p w k", k=WINDOW),
                                                               ACT.Identity, bias=bias(col, "qkv", n, r, e), scale=INV)
                                    a.then_inc(S["query_key_out"], 1)
                            elif stage == "value":
                                for n in range(VALUES):
                                    o = product_of(act, i, (stage, c, n))
                                    for r in range(2):
                                        a = act.activation(
                                            vexp_h[r * 64:r * 64 + 64, c, n * VROWS:n * VROWS + VROWS, r * HD:r * HD + HD],
                                            o[r * 64:r * 64 + 64, 0:VROWS * HD].rearrange("p (g x) -> p g x", x=HD),
                                            ACT.Copy)
                                    a.then_inc(S["v_hi"], 1)
                            elif stage == "score":
                                for p in range(PAIRS):
                                    act.wait_ge(S["score_out"], at("score_out", t, p))
                                    act.activation(prob[:, c, p, :, :], prob[:, c, p, :, :], ACT.Exp,
                                                   scale=HD ** -0.5).then_inc(S["prob_exp"], 1)
                            elif stage == "turn":
                                for p in range(PAIRS):
                                    o = product_of(act, i, (stage, c, p))
                                    act.activation(pt_h[:, p, :, :].rearrange("p a b -> p (a b)"), o[:, :], ACT.Copy).then_inc(S["turn_hi"], 1)
                            elif stage == "mix":
                                for p in range(PAIRS):
                                    f = keep((stage, c, p))
                                    o = product_of(act, i, (stage, c, p))
                                    for m in range(M):
                                        a = act.activation(f[:, m * P:m * P + P], o[:, m * P:m * P + P], ACT.Identity,
                                                           bias=bias(col, "qkv", 2 * M + m), scale=INV * INV)
                                    a.then_inc(S["mix_out"], 1)

                @block.vector
                def _(dve):
                    with dve.Fori(0, steps) as i:
                        def kept(key):
                            return full[:, full_at[key] % RING, :]

                        def split(src, hi, lo, hi_name, lo_name, t, n=0):
                            dve.tensor_copy(hi, src).then_inc(S[hi_name], 1)
                            dve.wait_ge(S[hi_name], at(hi_name, t, n))
                            dve.tensor_tensor(lo, src, hi, ALU.subtract).then_inc(S[lo_name], 1)

                        for stage, c in TOKENIZER:
                            t = CH * i + c
                            zc, rc = (x[:, c, :, :] for x in (z, res))
                            if stage == "patches":
                                dve.wait_ge(S["raw_hi"], at("raw_hi", t + CH))
                                dve.tensor_tensor(pat_l[:, c, :], raw[:, c, :], pat_h[:, c, :], ALU.subtract).then_inc(S["raw_lo"], 1)
                            elif stage == "mean":
                                o = product_of(dve, i, (stage, c, 0))
                                dve.tensor_tensor(zc, zc, o[:, 0:N].unsqueeze(1).broadcast_to([P, M, N]),
                                                  ALU.subtract).then_inc(S["mean_out"], 1)
                            elif stage == "var":
                                dve.wait_ge(S["var_out"], at("var_out", t))
                                dve.reciprocal(std[:, c, :], std[:, c, :]).then_inc(S["inverse"], 1)
                                dve.wait_ge(S["inverse"], at("inverse", t))
                                dve.tensor_tensor(zc, zc, std[:, c, :].unsqueeze(1).broadcast_to([P, M, N]),
                                                  ALU.mult).then_inc(S["normed"], 1)
                                dve.wait_ge(S["affine"], at("affine", t, M - 1))
                                dve.tensor_tensor(rc.rearrange("p m n -> p (m n)"), rc.rearrange("p m n -> p (m n)"),
                                                  table[:, c, :], ALU.add).then_inc(S["residual"], 1)
                                dve.wait_ge(S["residual"], at("residual", t))
                                split(rc, x_h[:, c, :, :], x_l[:, c, :, :], "x0_hi", "x0_lo", t)
                            elif stage in ("up0", "up1"):
                                for m in range(MH):
                                    dve.wait_ge(S[stage + "_out"], at(stage + "_out", t, m))
                                    split(kept((stage, c, m)), hid_h[:, c, m, :], hid_l[:, c, m, :], stage + "_hi", stage + "_lo", t, m)
                            elif stage == "down0":
                                for m in range(M):
                                    dve.wait_ge(S["down0_out"], at("down0_out", t, m))
                                    split(kept((stage, c, m)), x_h[:, c, m, :], x_l[:, c, m, :], "down0_hi", "down0_lo", t, m)
                            elif stage == "query_key":
                                for n in range(2 * M):
                                    dve.wait_ge(S["query_key_out"], at("query_key_out", t, n))
                                    f = kept((stage, c, n))
                                    if n < M:
                                        split(f, q_h[:, c, n, :], q_l[:, c, n, :], "q_hi", "q_lo", t, n)
                                        continue
                                    for h in range(4):
                                        r, e = h * HD, h * HD + HD
                                        d = dve.tensor_tensor(kexp_l[r:e, n - M, :, h, :],
                                                              f[r:e, :].rearrange("p (w k) -> p w k", k=WINDOW),
                                                              kexp_h[r:e, n - M, :, h, :], ALU.subtract)
                                    d.then_inc(S["k_lo"], 1)
                            elif stage == "value":
                                for n in range(VALUES):
                                    dve.wait_ge(S["v_hi"], at("v_hi", t, n))
                                    b, _ = placeA[(stage, c, n)]
                                    for r in range(2):
                                        to = [x[r * 64:r * 64 + 64, c, n * VROWS:n * VROWS + VROWS, r * HD:r * HD + HD] for x in (vexp_h, vexp_l)]
                                        d = dve.tensor_tensor(
                                            to[1], bank[b][r * 64:r * 64 + 64, 0:VROWS * HD].rearrange("p (g x) -> p g x", x=HD),
                                            to[0], ALU.subtract)
                                    d.then_inc(S["value_out"], 1)
                            elif stage == "score":
                                for p in range(PAIRS):
                                    o = product_of(dve, i, (stage, c, p)).rearrange("p (h k) -> p h k", h=HEADS)
                                    dve.tensor_reduce(top[:, c, p, :], o, AX_X, ALU.max).then_inc(S["score_top"], 1)
                                    dve.wait_ge(S["score_top"], at("score_top", t, p))
                                    dve.tensor_tensor(prob[:, c, p, :, :], o, top[:, c, p, :].unsqueeze(2).broadcast_to([P, HEADS, WINDOW]),
                                                      ALU.subtract).then_inc(S["score_out"], 1)
                                for p in range(PAIRS):
                                    pr, rr = prob[:, c, p, :, :], rec[:, c, p, :]
                                    dve.wait_ge(S["prob_exp"], at("prob_exp", t, p))
                                    dve.tensor_reduce(rr, pr, AX_X, ALU.add).then_inc(S["prob_sum"], 1)
                                    dve.wait_ge(S["prob_sum"], at("prob_sum", t, p))
                                    dve.reciprocal(rr, rr).then_inc(S["prob_rec"], 1)
                                    dve.wait_ge(S["prob_rec"], at("prob_rec", t, p))
                                    dve.scalar_tensor_tensor(pr, pr, WS, rr.unsqueeze(2).broadcast_to([P, HEADS, WINDOW]),
                                                             ALU.mult, ALU.mult).then_inc(S["prob_out"], 1)
                            elif stage == "turn":
                                for p in range(PAIRS):
                                    dve.wait_ge(S["turn_hi"], at("turn_hi", t, p))
                                    b, _ = placeA[(stage, c, p)]
                                    hi, lo = (x[:, p, :, :].rearrange("p a b -> p (a b)") for x in (pt_h, pt_l))
                                    dve.tensor_tensor(lo, bank[b][:, :], hi, ALU.subtract).then_inc(S["turn_out"], 1)
                            elif stage == "mix":
                                for p in range(PAIRS):
                                    dve.wait_ge(S["mix_out"], at("mix_out", t, p))
                                    split(kept((stage, c, p))[:, 0:M * P].rearrange("p (m n) -> p m n", m=M),
                                          x_h[:, c, :, p * P:p * P + P], x_l[:, c, :, p * P:p * P + P], "mix_hi", "mix_lo", t, p)
                            elif stage == "proj":
                                for m in range(M):
                                    dve.wait_ge(S["proj_out"], at("proj_out", t, m))
                                    dve.tensor_tensor(res[:, c, m, :], kept((stage, c, m)), res[:, c, m, :], ALU.add).then_inc(S["attended"], 1)
                                    dve.wait_ge(S["attended"], at("attended", t, m))
                                    if m == 0:
                                        product_of(dve, i, (stage, c, M - 1))
                                    split(res[:, c, m, :], x_h[:, c, m, :], x_l[:, c, m, :], "x1_hi", "x1_lo", t, m)
                            elif stage == "down1":
                                for m in range(M):
                                    dve.wait_ge(S["down1_out"], at("down1_out", t, m))
                                    dve.tensor_tensor(z[:, c, m, :], kept((stage, c, m)), res[:, c, m, :], ALU.add).then_inc(S["tokens_out"], 1)

        with ExitStack() as ctx:
            hin = sb(ctx, "hin", [P, M, SEQ])
            z = sb(ctx, "lz", [P, M, SEQ])
            sq = sb(ctx, "lsq", [P, M, SEQ])
            std = sb(ctx, "lstd", [P, SEQ])
            x_h = sb(ctx, "lx_h", [P, M, SEQ], F16)
            x_l = sb(ctx, "lx_l", [P, M, SEQ], F16)
            s_h = sb(ctx, "ls_h", [P, M, SEQ], F16)
            s_l = sb(ctx, "ls_l", [P, M, SEQ], F16)
            forget = sb(ctx, "forget", [P, M, SEQ])
            take = sb(ctx, "take", [P, M, SEQ])
            soft = sb(ctx, "soft", [P, M, SEQ])
            cand = sb(ctx, "cand", [P, M, SEQ])
            state = sb(ctx, "state", [P, 2, M, SEQ])
            res = sb(ctx, "lres", [P, M, SEQ])
            rh = sb(ctx, "rh", [P, SEQ])
            shape = [P, CH, TILES, EXPERTS]
            logit, mask1, mask2 = (sb(ctx, n, shape) for n in ("logit", "mask1", "mask2"))
            lim, rsum, gap, first_w, second_w = (sb(ctx, n, [P, CH, TILES]) for n in ("lim", "rsum", "gap", "first_w", "second_w"))
            chance = sb(ctx, "chance", [P, CH, TILES, 8])
            best = sb(ctx, "best", [P, CH, TILES, 8])
            best_at = sb(ctx, "best_at", [P, CH, TILES, 8], U32)
            best_f = sb(ctx, "best_f", [P, CH, TILES, 8])
            spare = sb(ctx, "spare", [P, 1])
            number = sb(ctx, "number", [P, TILES, EXPERTS])
            parts = sb(ctx, "parts", [P, CH, TILES, 2 * EXPERTS], F16)
            wt = sb(ctx, "wt", [2 * EXPERTS, SEQ + 3], F16)
            share = sb(ctx, "share", [P, EXPERTS, SEQ])
            full1 = sb(ctx, "full1", [P, 2, HALF[0]])
            full2 = sb(ctx, "full2", [P, 2, HALF[0]])
            h1_h = sb(ctx, "h1_h", [P, RING1, M, HALF[0]], F16)
            h1_l = sb(ctx, "h1_l", [P, RING1, M, HALF[0]], F16)
            h2_h = sb(ctx, "h2_h", [P, RING2, M, HALF[0]], F16)
            h2_l = sb(ctx, "h2_l", [P, RING2, M, HALF[0]], F16)
            ob = sb(ctx, "ob", [P, M, SEQ])
            layer_consts = sem("layer_consts")
            block = ctx.enter_context(nc.Block())

            base = [steps * usesA[b] for b in range(8)]
            sums = [bank[6], bank[7]]
            TB = 577
            order = layer_groups()

            def at(name, t, n=0):
                return count(LAYER_SIGNALS, name, t, n)

            def product_of(eng, i, key):
                b, k = placeB[key]
                eng.wait_ge(bank_full[b], i * usesB[b] + base[b] + k + 1)
                return bank[b]

            def cut(c):
                return slice(START[c], START[c] + HALF[c])

            @block.sync
            def _(sp):
                sp.dma_start(hin[:, :, 1:SEQ], tok[:, :, 0:PATCHES]).then_inc(tokens_loaded, 16)

                def store(i, c):
                    sp.wait_ge(L["combined"], at("combined", CH * i + c, M - 1))
                    sp.dma_start(out[:, :, bass.ds(i * SEQ + START[c], HALF[c])], ob[:, :, cut(c)]).then_inc(out_stored[c], 16)

                with sp.Fori(0, images - 1) as i:
                    sp.wait_ge(L["mixed"], at("mixed", CH * i + 1))
                    sp.dma_start(hin[:, :, 1:SEQ], tok[:, :, bass.ds((i + 1) * PATCHES, PATCHES)]).then_inc(tokens_loaded, 16)
                    for c in range(CH):
                        store(i, c)
                for c in range(CH):
                    store(images - 1, c)
                for c in range(CH):
                    sp.wait_ge(out_stored[c], 16 * images + 16)

            @block.gpsimd
            def _(pool):
                pool.memset(chance[:], -1.0).then_inc(layer_consts, 1)
                for e in range(EXPERTS):
                    pool.memset(number[:, :, e:e + 1], float(e)).then_inc(layer_consts, 1)

            @block.tensor
            def _(pe):
                pe.wait_ge(layer_consts, 2 + EXPERTS)
                with pe.Fori(0, images) as i:
                    def group(key, ready=None):
                        b, k = placeB[key]
                        n = order.index(key)
                        s, c, m = order[n - 6] if n >= 6 else order[[g for g in range(len(order)) if placeB[order[g]][0] == b][-1]]
                        if ready is not None:
                            pe.wait_ge(L[ready[0]], at(*ready))
                        if ready is None or ready[0] != s + "_out":
                            pe.wait_ge(L[s + "_out"], at(s + "_out", CH * i + c - (0 if n >= 6 else CH), m))
                        return bank[b], bank_full[b]

                    for stage, c in LAYER:
                        t = CH * i + c
                        w = HALF[c]
                        if stage[:-1] in ("mean", "var"):
                            if stage == "mean1":
                                pe.wait_ge(tokens_loaded, 16 * i + 16)
                                ready = None
                            else:
                                ready = ("mixed" if stage == "mean2" else "squared" + stage[-1], t)
                            src = {"mean1": hin, "mean2": res, "var1": sq, "var2": sq}[stage]
                            o, filled = group((stage, c, 0), ready)
                            for m in range(M):
                                mm = pe.matmul(o[:, 0:w], ones[:, :], src[:, m, cut(c)], start=(m == 0), stop=(m == M - 1))
                            mm.then_inc(filled, 1)
                        elif stage in ("gru0", "gru1"):
                            name = "norm1_lo" if stage == "gru0" else "state0_lo"
                            xs = (x_h, x_l) if stage == "gru0" else (s_h, s_l)
                            for n in range(2 * M):
                                o, filled = group((stage, c, n), (name, t) if n == 0 else None)
                                f = (n % 2) * M + n // 2
                                product(pe, o[:, 0:w], [
                                    ([weight(x, WB[stage], k, 2 * D, f * P, f * P + P) for x in (wbh, wbl)],
                                     [x[:, k, cut(c)] for x in xs]) for k in range(M)]).then_inc(filled, 1)
                        elif stage == "route":
                            o, filled = group(("router1", c, 0), ("norm2_lo", t))
                            product(pe, o[:, 0:w], [
                                ([weight(x, WB["router1"], k, ROUTER, 0, ROUTER) for x in (wbh, wbl)],
                                 [x[:, k, cut(c)] for x in (x_h, x_l)]) for k in range(M)]).then_inc(filled, 1)
                            o, filled = group(("router2", c, 0), ("router1_out", t))
                            for j in range(TILES):
                                a = START[c] + j * TSTEP
                                mm = pe.matmul(o[0:TILE[c], j * EXPERTS:(j + 1) * EXPERTS], rh[:, a:a + TILE[c]],
                                               col[:, BC["router2_w"]:BC["router2_w"] + EXPERTS], start=True, stop=True)
                            mm.then_inc(filled, 1)
                            o, filled = group(("weights", c, 0), ("route", t, ROUTE_STEPS - 1))
                            for j in range(TILES):
                                a = j * TSTEP
                                mm = pe.transpose(o[0:2 * EXPERTS, :].bitcast(F16)[:, a:a + TILE[c]],
                                                  parts[0:TILE[c], c, j, :], idh[0:TILE[c], 0:TILE[c]])
                            mm.then_inc(filled, 1)
                        elif stage == "share":
                            for e in range(EXPERTS):
                                o, filled = group((stage, c, e), ("weights_out", t) if e == 0 else None)
                                pe.matmul(o[:, 0:w], sel[:, e * P:e * P + P], wt[:, cut(c)], start=True, stop=True).then_inc(filled, 1)
                        elif stage == "experts":
                            for layer, e in expert_steps():
                                if layer == 1:
                                    xs = [[x[:, k, cut(c)] for x in (x_h, x_l)] for k in range(M)]
                                elif layer == 2:
                                    pe.wait_ge(L["h1_lo"], at("h1_lo", t, e * M + M - 1))
                                    xs = [[x[:, e % RING1, k, 0:w] for x in (h1_h, h1_l)] for k in range(M)]
                                else:
                                    pe.wait_ge(L["h2_lo"], at("h2_lo", t, e * M + M - 1))
                                    xs = [[x[:, e % RING2, k, 0:w] for x in (h2_h, h2_l)] for k in range(M)]
                                    if e == 0:
                                        pe.wait_ge(L["combined"], at("combined", t - 1, M - 1))
                                for m in range(M):
                                    ws = [[weight(x, WB["expert%d" % layer] + e * M * D, k, D, m * P, m * P + P) for x in (wbh, wbl)]
                                          for k in range(M)]
                                    if layer < 3:
                                        o, filled = group(("expert%d" % layer, c, e * M + m))
                                        product(pe, o[:, 0:w], list(zip(ws, xs))).then_inc(filled, 1)
                                        continue
                                    for k in range(M):
                                        for n, (a, b) in enumerate(((0, 0), (0, 1), (1, 0))):
                                            pe.matmul(sums[m][:, 0:w], ws[k][a], xs[k][b],
                                                      start=(e == 0 and k == 0 and n == 0), stop=False)
                                    if e == EXPERTS - 1:
                                        pe.matmul(sums[m][:, 0:w], b3h[:, m * P:m * P + P], wt[:, cut(c)], start=False, stop=False)
                                        pe.matmul(sums[m][:, 0:w], b3l[:, m * P:m * P + P], wt[:, cut(c)],
                                                  start=False, stop=True).then_inc(L["sums_full"], 1)

            @block.scalar
            def _(act):
                with act.Fori(0, images) as i:
                    for stage, c in LAYER:
                        t = CH * i + c
                        w = HALF[c]
                        if stage[:-1] == "mean":
                            k = stage[-1]
                            act.wait_ge(L[stage + "_out"], at(stage + "_out", t))
                            act.activation(sq[:, :, cut(c)], z[:, :, cut(c)], ACT.Square).then_inc(L["squared" + k], 1)
                        elif stage[:-1] == "var":
                            o = product_of(act, i, (stage, c, 0))
                            act.activation(std[:, cut(c)], o[:, 0:w], ACT.Sqrt, bias=epsc[:, 0:1]).then_inc(L[stage + "_out"], 1)
                        elif stage in ("gru0", "gru1"):
                            for n in range(2 * M):
                                o, m, f = product_of(act, i, (stage, c, n)), n // 2, (n % 2) * M + n // 2
                                if n % 2 == 0:
                                    act.activation(forget[:, m, cut(c)], o[:, 0:w], ACT.Sigmoid, bias=bias(ncol, stage, f), scale=-INV)
                                    act.activation(take[:, m, cut(c)], o[:, 0:w], ACT.Sigmoid, bias=bias(col, stage, f),
                                                   scale=INV).then_inc(L[stage + "_out"], 1)
                                else:
                                    act.activation(soft[:, m, cut(c)], o[:, 0:w], ACT.Sigmoid, bias=bias(col, stage, f), scale=INV)
                                    act.activation(cand[:, m, cut(c)], o[:, 0:w], ACT.Relu, bias=bias(col, stage, f),
                                                   scale=INV).then_inc(L[stage + "_out"], 1)
                        elif stage == "route":
                            o = product_of(act, i, ("router1", c, 0))
                            act.activation(rh[:, cut(c)], o[:, 0:w], ACT.Relu, bias=bias(col, "router1", 0),
                                           scale=INV).then_inc(L["router1_out"], 1)
                            lg = logit[0:TILE[c], c, :, :].rearrange("p a b -> p (a b)")
                            act.wait_ge(L["route"], at("route", t, 1))
                            act.activation(lg, lg, ACT.Exp).then_inc(L["router_exp"], 1)
                            act.wait_ge(L["route"], at("route", t, 8))
                            act.activation(gap[0:TILE[c], c, :], gap[0:TILE[c], c, :], ACT.Exp).then_inc(L["router_exp2"], 1)
                        elif stage == "share":
                            for e in range(EXPERTS):
                                o = product_of(act, i, (stage, c, e))
                                act.activation(share[:, e, cut(c)], o[:, 0:w], ACT.Copy).then_inc(L["share_out"], 1)
                        elif stage == "experts":
                            for layer, e in expert_steps():
                                if layer == 3:
                                    continue
                                name, used, ring = ("expert1", "h1_lo", full1) if layer == 1 else ("expert2", "h2_lo", full2)
                                for m in range(M):
                                    n = e * M + m
                                    act.wait_ge(L[used], at(used, t, n - 2))
                                    o = product_of(act, i, (name, c, n))
                                    act.activation(ring[:, m, 0:w], o[:, 0:w], ACT.Relu, bias=bias(col, name, n),
                                                   scale=INV).then_inc(L[name + "_out"], 1)

            @block.vector
            def _(dve):
                dve.tensor_copy(hin[:, :, 0:1], col[:, BC["cls"]:BC["cls"] + M].unsqueeze(2)).then_inc(layer_consts, 1)
                dve.wait_ge(layer_consts, 2 + EXPERTS)
                with dve.Fori(0, images) as i:
                    def split(src, hi, lo, hi_name, lo_name, t, n=0):
                        dve.tensor_copy(hi, src).then_inc(L[hi_name], 1)
                        dve.wait_ge(L[hi_name], at(hi_name, t, n))
                        dve.tensor_tensor(lo, src, hi, ALU.subtract).then_inc(L[lo_name], 1)

                    for stage, c in LAYER:
                        t = CH * i + c
                        w = HALF[c]
                        zc = z[:, :, cut(c)]
                        if stage[:-1] == "mean":
                            o = product_of(dve, i, (stage, c, 0))
                            src = hin if stage == "mean1" else res
                            dve.tensor_tensor(zc, src[:, :, cut(c)], o[:, 0:w].unsqueeze(1).broadcast_to([P, M, w]),
                                              ALU.subtract).then_inc(L[stage + "_out"], 1)
                        elif stage[:-1] == "var":
                            k = stage[-1]
                            dve.wait_ge(L[stage + "_out"], at(stage + "_out", t))
                            dve.reciprocal(std[:, cut(c)], std[:, cut(c)]).then_inc(L["inverse" + k], 1)
                            dve.wait_ge(L["inverse" + k], at("inverse" + k, t))
                            dve.tensor_tensor(zc, zc, std[:, cut(c)].unsqueeze(1).broadcast_to([P, M, w]),
                                              ALU.mult).then_inc(L["normed" + k], 1)
                            dve.wait_ge(L["normed" + k], at("normed" + k, t))
                            split(zc, x_h[:, :, cut(c)], x_l[:, :, cut(c)], "norm%s_hi" % k, "norm%s_lo" % k, t)
                        elif stage in ("gru0", "gru1"):
                            g = int(stage[-1])
                            for m in range(M):
                                ca, so, ta, fo = (x[:, m, cut(c)] for x in (cand, soft, take, forget))
                                dve.wait_ge(L[stage + "_out"], at(stage + "_out", t, 2 * m + 1))
                                dve.scalar_tensor_tensor(ca, so, 0.5, ca, ALU.min, ALU.add).then_inc(L["candidate%d" % g], 1)
                                dve.wait_ge(L["candidate%d" % g], at("candidate%d" % g, t, m))
                                dve.tensor_tensor(ca, ca, ta, ALU.mult).then_inc(L["taken%d" % g], 1)
                                dve.wait_ge(L["taken%d" % g], at("taken%d" % g, t, m))
                                if c == 0:
                                    before = 0.5
                                else:
                                    dve.wait_ge(L["state%d" % g], at("state%d" % g, t - 1, m))
                                    before = state[:, g, m, START[c] - 1:START[c]]
                                dve.tensor_tensor_scan(state[:, g, m, cut(c)], fo, ca, before, ALU.mult, ALU.add
                                                       ).then_inc(L["state%d" % g], 1)
                            dve.wait_ge(L["state%d" % g], at("state%d" % g, t, M - 1))
                            if g == 0:
                                split(state[:, 0, :, cut(c)], s_h[:, :, cut(c)], s_l[:, :, cut(c)], "state0_hi", "state0_lo", t)
                            else:
                                dve.tensor_tensor(res[:, :, cut(c)], state[:, 1, :, cut(c)], hin[:, :, cut(c)],
                                                  ALU.add).then_inc(L["mixed"], 1)
                        elif stage == "route":
                            q = TILE[c]
                            done = [0]

                            def step(d):
                                d.then_inc(L["route"], 1)
                                dve.wait_ge(L["route"], at("route", t, done[0]))
                                done[0] += 1

                            def wide(x):
                                return x.unsqueeze(2).broadcast_to([q, TILES, EXPERTS])

                            lg, m1, m2 = (x[0:q, c, :, :] for x in (logit, mask1, mask2))
                            lm, rs, gp, fw, sw = (x[0:q, c, :] for x in (lim, rsum, gap, first_w, second_w))
                            ch = chance[0:q, c, :, :]
                            o = product_of(dve, i, ("router2", c, 0))[0:q, 0:TILES * EXPERTS].rearrange("p (a b) -> p a b", a=TILES)
                            b2 = col[0:q, BC["router2"]:BC["router2"] + EXPERTS].unsqueeze(1).broadcast_to([q, TILES, EXPERTS])
                            dve.tensor_tensor(lg, o, b2, ALU.add).then_inc(L["router2_out"], 1)
                            dve.wait_ge(L["router2_out"], at("router2_out", t))
                            step(dve.tensor_reduce(lm, lg, AX_X, ALU.max))
                            step(dve.tensor_tensor(lg, lg, wide(lm), ALU.subtract))
                            dve.wait_ge(L["router_exp"], at("router_exp", t))
                            step(dve.tensor_reduce(rs, lg, AX_X, ALU.add))
                            step(dve.reciprocal(rs, rs))
                            step(dve.tensor_tensor(ch[:, :, 0:EXPERTS], lg, wide(rs), ALU.mult))
                            dve.tensor_copy(spare[0:q, :], ch[:, 0, 0:1])
                            for j in range(TILES):
                                d = dve.max(best[0:q, c, j, :], ch[:, j, :])
                            step(d)
                            dve.tensor_copy(spare[0:q, :], best[0:q, c, 0, 0:1])
                            for j in range(TILES):
                                d = dve.max_index(best_at[0:q, c, j, :], best[0:q, c, j, :], ch[:, j, :])
                            step(d)
                            step(dve.tensor_copy(best_f[0:q, c, :, :], best_at[0:q, c, :, :]))
                            step(dve.tensor_tensor(gp, best[0:q, c, :, 1], best[0:q, c, :, 0], ALU.subtract))
                            num = number[0:q, :, :]
                            step(dve.tensor_tensor(m1, num, wide(best_f[0:q, c, :, 0]), ALU.is_equal))
                            step(dve.tensor_tensor(m2, num, wide(best_f[0:q, c, :, 1]), ALU.is_equal))
                            dve.wait_ge(L["router_exp2"], at("router_exp2", t))
                            step(dve.tensor_scalar(fw, gp, 1.0, None, ALU.add))
                            step(dve.reciprocal(fw, fw))
                            step(dve.tensor_tensor(sw, gp, fw, ALU.mult))
                            step(dve.tensor_tensor(m1, m1, wide(fw), ALU.mult))
                            step(dve.tensor_tensor(m2, m2, wide(sw), ALU.mult))
                            step(dve.tensor_tensor(m1, m1, m2, ALU.add))
                            pa = parts[0:q, c, :, :]
                            step(dve.tensor_copy(pa[:, :, 0:EXPERTS], m1))
                            step(dve.tensor_tensor(pa[:, :, EXPERTS:2 * EXPERTS], m1, pa[:, :, 0:EXPERTS], ALU.subtract))
                            o = product_of(dve, i, ("weights", c, 0))[0:2 * EXPERTS, :].bitcast(F16)[:, 0:w]
                            dve.tensor_copy(wt[:, cut(c)], o).then_inc(L["weights_out"], 1)
                        elif stage == "experts":
                            for layer, e in expert_steps():
                                if layer == 3:
                                    continue
                                if e == 0 and layer == 2:
                                    dve.wait_ge(L["share_out"], at("share_out", t, EXPERTS - 1))
                                for m in range(M):
                                    n = e * M + m
                                    if layer == 1:
                                        dve.wait_ge(L["expert1_out"], at("expert1_out", t, n))
                                        split(full1[:, m, 0:w], h1_h[:, e % RING1, m, 0:w], h1_l[:, e % RING1, m, 0:w], "h1_hi", "h1_lo", t, n)
                                    else:
                                        dve.wait_ge(L["expert2_out"], at("expert2_out", t, n))
                                        dve.tensor_tensor(full2[:, m, 0:w], full2[:, m, 0:w], share[:, e, cut(c)], ALU.mult
                                                          ).then_inc(L["h2_weighted"], 1)
                                        dve.wait_ge(L["h2_weighted"], at("h2_weighted", t, n))
                                        split(full2[:, m, 0:w], h2_h[:, e % RING2, m, 0:w], h2_l[:, e % RING2, m, 0:w], "h2_hi", "h2_lo", t, n)
                            dve.wait_ge(out_stored[c], 16 * i + 16)
                            for m in range(M):
                                dve.wait_ge(L["sums_full"], at("sums_full", t, m))
                                dve.scalar_tensor_tensor(ob[:, m, cut(c)], sums[m][:, 0:w], INV, res[:, m, cut(c)],
                                                         ALU.mult, ALU.add).then_inc(L["combined"], 1)


def _by_input(w):
    k, n = w.shape
    return w.reshape(k // P, P, n).transpose(1, 0, 2).reshape(P, -1)


def _positions():
    place = np.arange(PATCHES, dtype=np.float32)[:, None]
    i = np.arange(0, D, 2, dtype=np.float32)
    angle = place * np.exp(-np.log(np.float32(10000.0)) * i / np.float32(D)).astype(np.float32)
    pe = np.stack([np.sin(angle), np.cos(angle)], axis=-1).reshape(PATCHES, D).astype(np.float32)
    every = np.tile(pe, (IMAGES, 1))
    return np.ascontiguousarray(every.reshape(TOKENS // N, N, M, P).transpose(0, 3, 2, 1).reshape(TOKENS // N, P, M * N))


def kernel(x, cls_tok, **w):
    import concourse.bacc as bacc
    from concourse.bass_utils import run_bass_kernel_spmd as run

    g = {k[3:]: np.asarray(v) for k, v in w.items()}
    side = SIDE // PATCH
    patches = np.asarray(x).reshape(IMAGES, CHANNELS, side, PATCH, side, PATCH).transpose(1, 3, 5, 0, 2, 4)
    patches = patches.reshape(KP, P, TOKENS // N, N).transpose(2, 1, 0, 3).reshape(TOKENS // N, P, KP * N)
    wa = np.concatenate([_by_input(g["tok_conv_w"].reshape(D, -1).T), _by_input(g["tok_ff_w1"].T), _by_input(g["tok_ff_w2"].T),
                         _by_input(g["tok_qkv_w"].T), _by_input(g["tok_proj_w"].T)], axis=1)
    wb = np.concatenate([_by_input(g["attn_W0"].T), _by_input(g["attn_W1"].T), _by_input(g["ffn_router_w1"])]
                        + [_by_input(g["ffn_expert_w%d" % k][e]) for k in (1, 2, 3) for e in range(EXPERTS)], axis=1)

    def tall(v):
        return v.reshape(-1, P).T

    rows = [tall(g["tok_" + n]) for n in ("conv_b", "ln_w", "ln_b", "ff_b1", "ff_b2", "qkv_b", "proj_b")]
    rows += [tall(g[n]) for n in ("attn_b0", "attn_b1", "ffn_router_b1", "ffn_expert_b1", "ffn_expert_b2")]
    rows += [np.tile(g["ffn_router_b2"], (P, 1)), g["ffn_router_w2"],
             tall(np.asarray(cls_tok))]
    b3 = np.zeros((2 * EXPERTS, D + EXPERTS * P), np.float32)
    b3[:EXPERTS, :D] = b3[EXPERTS:, :D] = g["ffn_expert_b3"]
    for e in range(EXPERTS):
        b3[[e, EXPERTS + e], D + e * P:D + e * P + P] = 1.0
    arrays = {
        "patches": patches, "positions": _positions(), "tokenizer_weights": wa, "layer_weights": wb,
        "columns": np.concatenate(rows, axis=1), "last_bias": b3,
        "identity": np.eye(P, dtype=np.float32),
    }
    arrays = {k: np.ascontiguousarray(v) for k, v in arrays.items()}
    nc = bacc.Bacc("TRN2", target_bir_lowering=False, num_devices=1)
    args = [nc.dram_tensor(k, a.shape, mybir.dt.from_np(a.dtype), kind="ExternalInput").ap() for k, a in arrays.items()]
    args.append(nc.dram_tensor("out", (P, M, IMAGES * SEQ), F32, kind="ExternalOutput").ap())
    build_program(nc, *args)
    r = run(nc, [arrays], core_ids=[0])
    return r.results[0]["out"].reshape(P, M, IMAGES, SEQ).transpose(2, 3, 1, 0).reshape(IMAGES, SEQ, D)
```

```python
from contextlib import ExitStack

import numpy as np

import concourse.bass as bass
from concourse import mybir

ALU = mybir.AluOpType
ACT = mybir.ActivationFunctionType
AX_X = mybir.AxisListType.X
F32 = mybir.dt.float32
F16 = mybir.dt.float16
U32 = mybir.dt.uint32

P = 128
IMAGES, CHANNELS, SIDE, PATCH = 16, 3, 384, 16
D = 256
M = D // P
PATCHES = (SIDE // PATCH) ** 2
TOKENS = IMAGES * PATCHES
SEQ = PATCHES + 1
KP = CHANNELS * PATCH * PATCH // P
HF = 1024
MH = HF // P
HEADS, WINDOW = 8, 64
HD = D // HEADS
EXPERTS = 6
ROUTER = D // 2

N = 384
CH = 2
STEPS = TOKENS // (N * CH)
PAIRS = N // (2 * WINDOW)
WINDOWS = N // WINDOW
VALUES = 2
VROWS = WINDOWS // VALUES * 4
POSITIONS = 3
assert (N * POSITIONS) % PATCHES == 0

HALF = [SEQ - SEQ // 2, SEQ // 2]
START = [0, HALF[0]]
TILES = 3
TILE = [HALF[0] // TILES + 1, HALF[1] // TILES]
TSTEP = HALF[1] // TILES

WS = 64.0
INV = 1.0 / WS
EPS = 1e-5

def _columns(sizes):
    at, out = 0, {}
    for name, size in sizes:
        out[name] = at
        at += size
    return out, at


WA, WA_COLS = _columns([("conv", KP * D), ("ff1", M * HF), ("ff2", MH * D), ("qkv", M * 3 * D), ("proj", M * D)])
WB, WB_COLS = _columns([("gru0", M * 2 * D), ("gru1", M * 2 * D), ("router1", M * ROUTER),
                        ("expert1", EXPERTS * M * D), ("expert2", EXPERTS * M * D), ("expert3", EXPERTS * M * D)])
BC, BC_COLS = _columns([("conv", M), ("ln_w", M), ("ln_b", M), ("ff1", MH), ("ff2", M), ("qkv", 3 * M), ("proj", M),
                        ("gru0", 2 * M), ("gru1", 2 * M), ("router1", 1), ("expert1", EXPERTS * M),
                        ("expert2", EXPERTS * M), ("router2", EXPERTS), ("router2_w", EXPERTS), ("cls", M)])
WA_PARTS = [(0, KP * D), (WA["ff1"], M * HF), (WA["ff2"], MH * D), (WA["qkv"], M * 3 * D), (WA["proj"], M * D)]


GROUPS = {"patches": 1, "conv": M, "var": 1, "rstd": 1, "up0": MH, "up1": MH, "down0": M, "down1": M,
          "query_key": 2 * M, "value": VALUES, "score": PAIRS, "turn": PAIRS, "mix": PAIRS, "proj": M}


def entry(stage, c, lo=0, hi=None, ahead=0):
    return stage, c, lo, GROUPS[stage] if hi is None else hi, ahead


TOKENIZER = [
    entry("up0", 1, 0, 3), entry("down0", 0), entry("up0", 1, 3, 5), entry("query_key", 0), entry("value", 0),
    entry("up0", 1, 5, 8), entry("score", 0), entry("down0", 1, 0, 1), entry("patches", 0, ahead=1),
    entry("down0", 1, 1, 2), entry("turn", 0), entry("mix", 0), entry("query_key", 1), entry("proj", 0),
    entry("value", 1), entry("score", 1), entry("up1", 0, 0, 6), entry("turn", 1), entry("up1", 0, 6, 8),
    entry("mix", 1), entry("down1", 0, 0, 1), entry("proj", 1), entry("down1", 0, 1, 2),
    entry("patches", 1, ahead=1), entry("conv", 0, ahead=1), entry("up1", 1, 0, 2), entry("var", 0, ahead=1),
    entry("up1", 1, 2, 8), entry("rstd", 0, ahead=1), entry("down1", 1), entry("conv", 1, ahead=1),
    entry("up0", 0, 0, 1, ahead=1), entry("var", 1, ahead=1), entry("up0", 0, 1, 4, ahead=1),
    entry("rstd", 1, ahead=1), entry("up0", 0, 4, 8, ahead=1),
]

GROUPS.update({"tokens": 0, "mean1": 1, "var1": 1, "rstd1": 1, "gru0": 2 * M, "gru1": 2 * M, "mixed": 0, "mean2": 1,
               "var2": 1, "rstd2": 1, "router1": 1, "router2": 1, "weights": 1, "share": EXPERTS})
LAG2, LAG3 = 1, 2


def expert_steps():
    for n in range(EXPERTS + LAG3):
        if n < EXPERTS:
            yield 1, n
        if 0 <= n - LAG2 < EXPERTS:
            yield 2, n - LAG2
        if 0 <= n - LAG3 < EXPERTS:
            yield 3, n - LAG3


def layer_phase(c, routed_ahead):
    r = 1 - c
    between = {
        0: [entry("mixed", r, ahead=routed_ahead)],
        1: [entry("tokens", c, ahead=1)],
        2: [entry("mean1", c, ahead=1), entry("mean2", r, ahead=routed_ahead)],
        4: [entry("var1", c, ahead=1)],
        5: [entry("var2", r, ahead=routed_ahead)],
        6: [entry("rstd1", c, ahead=1)],
        7: [entry("rstd2", r, ahead=routed_ahead)],
        8: [entry("gru0", c, 0, 2, ahead=1), entry("gru0", c, 2, 4, ahead=1)],
        10: [entry("router1", r, ahead=routed_ahead)],
        11: [entry("router2", r, ahead=routed_ahead)],
        14: [entry("gru1", c, 0, 2, ahead=1), entry("weights", r, ahead=routed_ahead)],
        15: [entry("gru1", c, 2, 4, ahead=1)],
        16: [entry("share", r, ahead=routed_ahead)],
    }
    out = []
    for n, (layer, e) in enumerate(expert_steps()):
        out += [("expert%d" % layer, c, e * M, e * M + M, 0)] + between.get(n, [])
    return out


LAYER = layer_phase(0, 0) + layer_phase(1, 1)


def parts_of(body):
    return {"first": [e for e in body if e[4]], "body": body, "last": [e for e in body if not e[4]]}


def rotate(body, places, repeats, start=None, has=lambda stage, n: True):
    filled = dict(start or {p: 0 for p in places})
    plans = {}
    sequences = {part: [(s, c, n, a) for s, c, lo, hi, a in es for n in range(lo, hi) if has(s, n)]
                 for part, es in parts_of(body).items()}
    ends = {}
    for k, g in enumerate(sequences["body"]):
        ends[places[k % len(places)]] = g
    for part, seq in sequences.items():
        uses = {p: sum(k % len(places) == j for k in range(len(seq))) for j, p in enumerate(places)}
        plan = {}
        for k, (s, c, n, a) in enumerate(seq):
            p = places[k % len(places)]
            if k >= len(places):
                before = seq[k - len(places)]
            elif part == "first":
                before = None
            else:
                before = ends[p][:3] + (ends[p][3] - 1,)
            plan[s, c, n] = (p, filled[p] + k // len(places), uses[p] if part == "body" else 0, before)
        plans[part] = plan
        for p in places:
            filled[p] += uses[p] * (repeats - 1 if part == "body" else 1)
    return plans, filled


TOKENIZER_SIGNALS = {
    "raw_hi": 1, "raw_lo": 1, "conv_out": M, "var_out": 1, "inverse": 1, "rstd_out": 1,
    "table_biased": M, "residual": M, "x0_hi": 1, "x0_lo": 1, "up0_out": MH, "up0_hi": MH, "up0_lo": MH // 2, "up0_lo_odd": MH // 2, "down0_out": M,
    "down0_hi": M, "down0_lo": M, "query_key_out": 2 * M, "q_hi": M, "q_lo": M, "k_lo": M, "v_hi": VALUES,
    "value_out": VALUES, "score_top": PAIRS, "score_out": PAIRS, "prob_exp": PAIRS, "prob_sum": PAIRS,
    "prob_rec": PAIRS, "prob_out": PAIRS, "turn_hi": PAIRS, "turn_out": PAIRS, "mix_out": PAIRS, "mix_hi": PAIRS,
    "mix_lo": PAIRS, "proj_out": M, "attended": M, "x1_hi": M, "x1_lo": M, "up1_out": MH, "up1_hi": MH,
    "up1_lo": MH // 2, "up1_lo_odd": MH // 2, "down1_out": M, "tokens_out": M,
}
FULL_USERS = {"query_key": None, "up0": None, "up1": None, "down0": "down0_lo", "mix": "mix_lo", "proj": "attended",
              "down1": "tokens_out"}
RING = 4


def low_signal(stage, m):
    return stage + ("_lo_odd" if m % 2 else "_lo"), m // 2


def full_signal(stage, n):
    if stage == "query_key":
        return ("q_lo", n) if n < M else ("k_lo", n - M)
    if stage in ("up0", "up1"):
        return low_signal(stage, n)
    return FULL_USERS[stage], n


ROUTE_STEPS = 19
LAYER_SIGNALS = {
    "token_hi": 1, "token_lo": 1, "mixed_hi": 1, "mixed_lo": 1,
    "mean1_out": 1, "squared1": 1, "summed1": 1, "var1_out": 1, "inverse1": 1, "rstd1_out": 1, "norm1_hi": 1, "norm1_lo": 1,
    "gru0_out": 2 * M, "gru1_out": 2 * M, "candidate0": M, "candidate1": M, "taken0": M, "taken1": M,
    "state0": M, "state1": M, "state0_hi": 1, "state0_lo": 1, "mixed": 1,
    "mean2_out": 1, "squared2": 1, "summed2": 1, "var2_out": 1, "inverse2": 1, "rstd2_out": 1, "norm2_hi": 1, "norm2_lo": 1,
    "router1_out": 1, "router2_out": 1, "route": ROUTE_STEPS, "router_exp": 1, "router_exp2": 1, "weights_out": 1,
    "share_out": EXPERTS, "expert1_out": EXPERTS * M, "h1_lo": EXPERTS * M,
    "expert2_out": EXPERTS * M, "h2_weighted": EXPERTS * M, "h2_hi": EXPERTS * M, "h2_lo": EXPERTS * M,
    "sums_full": M, "combined": M,
}
RING1, RING2 = LAG2 + 1, LAG3 - LAG2 + 1


def build_program(nc, patches, pos, wa, wb, cols, b3, ident, out, images=IMAGES):
    steps = images * PATCHES // (N * CH)
    wb_part = WB_COLS // (CH * steps)
    assert wb_part * CH * steps == WB_COLS
    tok = nc.dram_tensor("tokens_dram", (P, M, TOKENS), F32, kind="Internal").ap()

    with ExitStack() as whole:
        def sb(ctx, name, shape, dt=F32):
            return ctx.enter_context(nc.sbuf_tensor(name, shape, dt))

        def sem(name):
            return whole.enter_context(nc.semaphore(name))

        wah = sb(whole, "wah", [P, WA_COLS], F16)
        wal = sb(whole, "wal", [P, WA_COLS], F16)
        wbh = sb(whole, "wbh", [P, WB_COLS], F16)
        wbl = sb(whole, "wbl", [P, WB_COLS], F16)
        col = sb(whole, "col", [P, BC_COLS])
        ncol = sb(whole, "ncol", [P, BC_COLS])
        epsc = sb(whole, "epsc", [P, 1])
        scale = sb(whole, "scale", [P, 1])
        ones = sb(whole, "ones", [P, P])
        idf = sb(whole, "idf", [P, P])
        idh = sb(whole, "idh", [P, P], F16)
        b3raw = sb(whole, "b3raw", [2 * EXPERTS, D + EXPERTS * P])
        b3h = sb(whole, "b3h", [2 * EXPERTS, D], F16)
        b3l = sb(whole, "b3l", [2 * EXPERTS, D], F16)
        sel = sb(whole, "sel", [2 * EXPERTS, EXPERTS * P], F16)
        wbraw = sb(whole, "wbraw", [P, wb_part])
        bank = [whole.enter_context(nc.psum_tensor("bank%d" % b, [P, 512], F32)) for b in range(8)]

        consts_loaded, consts_made = sem("consts_loaded"), sem("consts_made")
        wa_loaded = [sem("wa_loaded%d" % n) for n in range(len(WA_PARTS))]
        wa_hi, wa_lo = sem("wa_hi"), sem("wa_lo")
        wb_loaded, wb_scaled, wb_hi, wb_lo = (sem("wb_" + s) for s in ("loaded", "scaled", "hi", "lo"))
        bank_full = [sem("bank_full%d" % b) for b in range(8)]
        raw_loaded = [sem("raw_loaded%d" % c) for c in range(CH)]
        table_loaded = [sem("table_loaded%d" % c) for c in range(CH)]
        tokens_stored = [sem("tokens_stored%d" % c) for c in range(CH)]
        S = {n: sem(n) for n in TOKENIZER_SIGNALS}
        half_loaded = [sem("half_loaded%d" % c) for c in range(CH)]
        out_stored = [sem("out_stored%d" % c) for c in range(CH)]
        L = {n: sem(n) for n in LAYER_SIGNALS}

        def count(signals, name, t, n=0):
            return signals[name] * (t + CH) + n + 1

        def weight(block, base, k, width, a, b):
            return block[:, base + k * width + a:base + k * width + b]

        def bias(table, name, m, a=0, b=P):
            return table[a:b, BC[name] + m:BC[name] + m + 1]

        def product(pe, o, terms):
            for k, ((wh, wl), (xh, xl)) in enumerate(terms):
                pe.matmul(o, wh, xh, start=(k == 0), stop=False)
                pe.matmul(o, wh, xl, start=False, stop=False)
                mm = pe.matmul(o, wl, xh, start=False, stop=(k == len(terms) - 1))
            return mm

        plan_a, filled = rotate(TOKENIZER, list(range(8)), steps, has=lambda stage, n: stage != "patches")
        plan_b, _ = rotate(LAYER, list(range(6)), images, filled, has=lambda stage, n: stage != "expert3")
        plan_full, _ = rotate(TOKENIZER, list(range(RING)), steps, has=lambda stage, n: stage in FULL_USERS)

        def run_parts(eng, repeats, part, settle=None):
            part(-1, "first")
            if settle is not None:
                settle()
            with eng.Fori(0, repeats - 1) as i:
                part(i, "body")
            part(repeats - 1, "last")

        with ExitStack() as ctx:
            raw = sb(ctx, "raw", [P, CH, KP * N])
            table = sb(ctx, "table", [P, CH, M * N])
            pat_h = sb(ctx, "pat_h", [P, CH, KP * N], F16)
            pat_l = sb(ctx, "pat_l", [P, CH, KP * N], F16)
            z = sb(ctx, "z", [P, CH, M, N])
            res = sb(ctx, "res", [P, CH, M, N])
            vexp_h = sb(ctx, "vexp_h", [P, CH, WINDOWS * 4, 2 * HD], F16)
            vexp_l = sb(ctx, "vexp_l", [P, CH, WINDOWS * 4, 2 * HD], F16)
            kexp_h = sb(ctx, "kexp_h", [P, M, WINDOWS, 4, WINDOW], F16)
            kexp_l = sb(ctx, "kexp_l", [P, M, WINDOWS, 4, WINDOW], F16)

            def patches_high(act, step, c):
                act.wait_ge(raw_loaded[c], 16 * step + 16)
                act.activation(pat_h[:, c, :], raw[:, c, :], ACT.Copy).then_inc(S["raw_hi"], 1)

            def patches_low(pool, step, c):
                pool.wait_ge(S["raw_hi"], count(TOKENIZER_SIGNALS, "raw_hi", CH * step + c))
                pool.tensor_tensor(pat_l[:, c, :], raw[:, c, :], pat_h[:, c, :], ALU.subtract).then_inc(S["raw_lo"], 1)
                pool.wait_ge(table_loaded[c], 16 * step + 16)
                for m in range(M):
                    part = slice(m * N, m * N + N)
                    pool.tensor_tensor(table[:, c, part], table[:, c, part], bias(col, "ln_b", m).broadcast_to([P, N]),
                                       ALU.add).then_inc(S["table_biased"], 1)

            with ExitStack() as first:
                wraw = sb(first, "wraw", [P, 2, M * HF])
                wmean = sb(first, "wmean", [P, KP])
                centered, bias_mean, bias_centered = sem("centered"), sem("bias_mean"), sem("bias_centered")
                block = first.enter_context(nc.Block())

                @block.sync
                def _(sp):
                    sp.dma_start(wraw[:, 0, 0:WA_PARTS[0][1]], wa[:, 0:WA_PARTS[0][1]]).then_inc(wa_loaded[0], 16)
                    for src, dst in ((cols, col[:, :]), (ident, idf[:, :]), (b3, b3raw[:, :])):
                        sp.dma_start(dst, src).then_inc(consts_loaded, 16)
                    for n, (a, size) in enumerate(WA_PARTS):
                        if n == 0:
                            continue
                        if n >= 2:
                            sp.wait_ge(wa_lo, n - 1)
                        sp.dma_start(wraw[:, n % 2, 0:size], wa[:, a:a + size]).then_inc(wa_loaded[n], 16)
                        if n in (1, 3):
                            c = n // 2
                            sp.dma_start(raw[:, c, :], patches[c]).then_inc(raw_loaded[c], 16)
                            sp.dma_start(table[:, c, :], pos[c]).then_inc(table_loaded[c], 16)

                @block.tensor
                def _(pe):
                    pe.wait_ge(consts_made, 1)
                    pe.wait_ge(consts_loaded, 48)
                    pe.matmul(bank[0][:, 0:M], ones[:, :], col[:, BC["conv"]:BC["conv"] + M], start=True, stop=True
                              ).then_inc(bias_mean, 1)

                @block.scalar
                def _(act):
                    for n, (a, size) in enumerate(WA_PARTS):
                        if n == 0:
                            act.wait_ge(centered, 2)
                        else:
                            act.wait_ge(wa_loaded[n], 16)
                        act.activation(wah[:, a:a + size], wraw[:, n % 2, 0:size], ACT.Copy, scale=WS).then_inc(wa_hi, 1)
                        if n == 1:
                            patches_high(act, 0, 0)

                @block.vector
                def _(dve):
                    for name, per in TOKENIZER_SIGNALS.items():
                        dve.sem_inc(S[name], per * CH)
                    for name, per in LAYER_SIGNALS.items():
                        dve.sem_inc(L[name], per * CH)
                    for c in range(CH):
                        dve.sem_inc(tokens_stored[c], 16)
                        dve.sem_inc(out_stored[c], 16)
                    dve.sem_inc(wb_lo, 1)
                    conv_w = wraw[:, 0, 0:KP * D].rearrange("p (k o) -> p k o", o=D)
                    dve.wait_ge(wa_loaded[0], 16)
                    dve.tensor_reduce(wmean[:, :], conv_w, AX_X, ALU.add).then_inc(centered, 1)
                    dve.wait_ge(centered, 1)
                    dve.scalar_tensor_tensor(conv_w, wmean[:, :].unsqueeze(2).broadcast_to([P, KP, D]), -1.0 / D, conv_w,
                                             ALU.mult, ALU.add).then_inc(centered, 1)
                    conv_b = col[:, BC["conv"]:BC["conv"] + M]
                    for m in range(M):
                        if m == 0:
                            dve.wait_ge(bias_mean, 1)
                        else:
                            dve.wait_ge(bias_centered, m)
                        dve.tensor_scalar(conv_b, conv_b, bank[0][:, m:m + 1], None, ALU.subtract).then_inc(bias_centered, 1)
                    for n, (a, size) in enumerate(WA_PARTS):
                        dve.wait_ge(wa_hi, n + 1)
                        dve.scalar_tensor_tensor(wal[:, a:a + size], wraw[:, n % 2, 0:size], WS, wah[:, a:a + size],
                                                 ALU.mult, ALU.subtract).then_inc(wa_lo, 1)

                @block.gpsimd
                def _(pool):
                    pool.memset(ones[:, :], 1.0 / D).then_inc(consts_made, 1)
                    pool.memset(epsc[:, :], EPS).then_inc(consts_made, 1)
                    pool.memset(scale[:, :], WS).then_inc(consts_made, 1)
                    for t in (kexp_h, kexp_l, vexp_h, vexp_l):
                        pool.memset(t[:], 0.0).then_inc(consts_made, 1)
                    pool.wait_ge(consts_loaded, 48)
                    gates = slice(BC["gru0"], BC["gru1"] + 2 * M)
                    pool.tensor_scalar(ncol[:, gates], col[:, gates], -1.0, None, ALU.mult).then_inc(consts_made, 1)
                    pool.tensor_copy(idh[:, :], idf[:, :]).then_inc(consts_made, 1)
                    pool.tensor_copy(sel[:, :], b3raw[:, D:D + EXPERTS * P]).then_inc(consts_made, 1)
                    pool.tensor_scalar(b3raw[:, 0:D], b3raw[:, 0:D], WS, None, ALU.mult).then_inc(consts_made, 1)
                    pool.wait_ge(consts_made, 11)
                    pool.tensor_copy(b3h[:, :], b3raw[:, 0:D]).then_inc(consts_made, 1)
                    pool.wait_ge(consts_made, 12)
                    pool.tensor_tensor(b3l[:, :], b3raw[:, 0:D], b3h[:, :], ALU.subtract).then_inc(consts_made, 1)
                    patches_low(pool, 0, 0)

            with ExitStack() as second:
                hid_h = sb(second, "hid_h", [P, CH, MH, N], F16)
                hid_l = sb(second, "hid_l", [P, CH, MH, N], F16)
                x_h = sb(second, "x_h", [P, CH, M, N], F16)
                x_l = sb(second, "x_l", [P, CH, M, N], F16)
                dev = sb(second, "dev", [P, CH, PAIRS])
                full = sb(second, "full", [P, RING, N])
                q_h, q_l = hid_l[:, :, 0:M, :], hid_l[:, :, M:2 * M, :]
                prob = hid_h[:, :, :, :].rearrange("p c m n -> p (c m n)").bitcast(F32).rearrange(
                    "p (c a h k) -> p c a h k", c=CH, a=PAIRS, h=HEADS)
                pt_h = sb(second, "pt_h", [P, PAIRS, 4, P], F16)
                pt_l = sb(second, "pt_l", [P, PAIRS, 4, P], F16)
                top = sb(second, "top", [P, CH, PAIRS, HEADS])
                rec = sb(second, "rec", [P, CH, PAIRS, HEADS])
                block = second.enter_context(nc.Block())

                def at(name, t, n=0):
                    return count(TOKENIZER_SIGNALS, name, t, n)

                def product_of(eng, i, part, key):
                    b, k, step, _ = plan_a[part][key]
                    eng.wait_ge(bank_full[b], i * step + k + 1)
                    return bank[b]

                @block.sync
                def _(sp):
                    with sp.Fori(0, steps - 1) as i:
                        for c in range(CH):
                            sp.wait_ge(S["raw_lo"], at("raw_lo", CH * i + c))
                            sp.dma_start(raw[:, c, :], patches[bass.ds(CH * i + CH + c, 1)].rearrange("a p n -> (a p) n")
                                         ).then_inc(raw_loaded[c], 16)
                        for c in range(CH):
                            sp.wait_ge(S["residual"], at("residual", CH * i + c, M - 1))
                            sp.dma_start(table[:, c, :], pos[bass.ds(CH * i + CH + c, 1)].rearrange("a p n -> (a p) n")
                                         ).then_inc(table_loaded[c], 16)
                        for c in range(CH):
                            sp.wait_ge(S["tokens_out"], at("tokens_out", CH * i + c, M - 1))
                            sp.dma_start(tok[:, :, bass.ds((CH * i + c) * N, N)], z[:, c, :, :]).then_inc(tokens_stored[c], 16)
                    for c in range(CH):
                        sp.wait_ge(S["tokens_out"], at("tokens_out", CH * (steps - 1) + c, M - 1))
                        sp.dma_start(tok[:, :, (CH * (steps - 1) + c) * N:(CH * steps - CH + c + 1) * N], z[:, c, :, :]
                                     ).then_inc(tokens_stored[c], 16)
                    for c in range(CH):
                        sp.wait_ge(tokens_stored[c], 16 * steps + 16)

                @block.gpsimd
                def _(pool):
                    def stages(i, part):
                        for stage, c, lo, hi, ahead in parts_of(TOKENIZER)[part]:
                            t = CH * (i + ahead) + c
                            if stage == "patches":
                                if part != "first" or c > 0:
                                    patches_low(pool, i + ahead, c)
                            elif stage in ("up0", "up1"):
                                for m in range(lo, hi):
                                    if m % 2 == 1:
                                        pool.wait_ge(S[stage + "_hi"], at(stage + "_hi", t, m))
                                        pool.tensor_tensor(hid_l[:, c, m, :], full[:, plan_full[part][stage, c, m][0], :],
                                                           hid_h[:, c, m, :], ALU.subtract).then_inc(S[stage + "_lo_odd"], 1)
                            elif stage == "down1":
                                for m in range(lo, hi):
                                    pool.wait_ge(S["down1_out"], at("down1_out", t, m))
                                    pool.tensor_tensor(z[:, c, m, :], full[:, plan_full[part][stage, c, m][0], :], res[:, c, m, :],
                                                       ALU.add).then_inc(S["tokens_out"], 1)
                            elif stage == "query_key":
                                pool.wait_ge(wb_lo, t + 1)
                                pool.dma_start(wbraw[:, :], wb[:, bass.ds(t * wb_part, wb_part)]).then_inc(wb_loaded, 16)
                            elif stage == "value":
                                pool.wait_ge(wb_loaded, 16 * t + 16)
                                pool.tensor_tensor(wbraw[:, :], wbraw[:, :], scale[:, 0:1].broadcast_to([P, wb_part]),
                                                   ALU.mult).then_inc(wb_scaled, 1)
                            elif stage == "score":
                                pool.wait_ge(wb_scaled, t + 1)
                                pool.tensor_copy(wbh[:, bass.ds(t * wb_part, wb_part)], wbraw[:, :]).then_inc(wb_hi, 1)
                            elif stage == "turn":
                                pool.wait_ge(wb_hi, t + 1)
                                cut = bass.ds(t * wb_part, wb_part)
                                pool.tensor_tensor(wbl[:, cut], wbraw[:, :], wbh[:, cut], ALU.subtract).then_inc(wb_lo, 1)

                    run_parts(pool, steps, stages)

                @block.tensor
                def _(pe):
                    def stages(i, part):
                        def group(key, ready=None):
                            b, _, _, before = plan_a[part][key]
                            s = None if before is None else before[0]
                            if ready is not None:
                                pe.wait_ge(S[ready[0]], at(*ready))
                            if s is not None and (ready is None or ready[0] != s + "_out"):
                                pe.wait_ge(S[s + "_out"], at(s + "_out", CH * (i + before[3]) + before[1], before[2]))
                            return bank[b], bank_full[b]

                        def linear(stage, c, lo, hi, ready, name, ktiles, width, xh, xl):
                            for m in range(lo, hi):
                                o, filled = group((stage, c, m), ready if m == lo else None)
                                product(pe, o[:, 0:N], [
                                    ([weight(w, WA[name], k, width, m * P, m * P + P) for w in (wah, wal)], (xh(k), xl(k)))
                                    for k in range(ktiles)]).then_inc(filled, 1)

                        for stage, c, lo, hi, ahead in parts_of(TOKENIZER)[part]:
                            t = CH * (i + ahead) + c
                            xs = (lambda k, c=c: x_h[:, c, k, :]), (lambda k, c=c: x_l[:, c, k, :])
                            if stage == "conv":
                                linear(stage, c, lo, hi, ("raw_lo", t), "conv", KP, D, lambda k: pat_h[:, c, k * N:(k + 1) * N],
                                       lambda k: pat_l[:, c, k * N:(k + 1) * N])
                            elif stage == "var":
                                o, filled = group((stage, c, 0), ("conv_out", t, M - 1))
                                for j in range(PAIRS):
                                    for m in range(M):
                                        mm = pe.matmul(o[:, j:j + 1], res[:, c, m, j * P:j * P + P], ones[:, 0:1],
                                                       start=(m == 0), stop=(m == M - 1))
                                mm.then_inc(filled, 1)
                            elif stage == "rstd":
                                o, filled = group((stage, c, 0), ("inverse", t))
                                for j in range(PAIRS):
                                    mm = pe.matmul(o[:, j * P:j * P + P], dev[:, c, j:j + 1].broadcast_to([P, P]), idf[:, :],
                                                   start=True, stop=True)
                                mm.then_inc(filled, 1)
                            elif stage in ("up0", "up1"):
                                ready = ("x0_lo", t) if stage == "up0" else ("x1_lo", t, M - 1)
                                linear(stage, c, lo, hi, ready, "ff1", M, HF, *xs)
                            elif stage in ("down0", "down1"):
                                up = "up" + stage[-1]
                                pe.wait_ge(S[up + "_lo"], at(up + "_lo", t, MH // 2 - 1))
                                ready = (up + "_lo_odd", t, MH // 2 - 1)
                                linear(stage, c, lo, hi, ready, "ff2", MH, D, lambda k: hid_h[:, c, k, :], lambda k: hid_l[:, c, k, :])
                            elif stage == "query_key":
                                linear(stage, c, lo, hi, ("down0_lo", t, M - 1), "qkv", M, 3 * D, *xs)
                            elif stage == "value":
                                for n in range(lo, hi):
                                    o, filled = group((stage, c, n))
                                    for w in range(WINDOWS // VALUES):
                                        a = (n * (WINDOWS // VALUES) + w) * WINDOW
                                        for r in range(2):
                                            mm = product(pe, o[r * 64:r * 64 + 64, w * P:w * P + P], [
                                                ([x[:, c, k, a:a + WINDOW] for x in (x_h, x_l)],
                                                 [weight(x, WA["qkv"], k, 3 * D, 2 * D, 3 * D).rearrange("p (g x) -> p g x", g=4)[:, :, r * HD:r * HD + HD]
                                                  for x in (wah, wal)])
                                                for k in range(M)])
                                    mm.then_inc(filled, 1)
                            elif stage == "score":
                                pe.wait_ge(S["q_lo"], at("q_lo", t, M - 1))
                                pe.wait_ge(S["k_lo"], at("k_lo", t, M - 1))
                                for p in range(lo, hi):
                                    o, filled = group((stage, c, p))
                                    for w in range(2):
                                        a = (2 * p + w) * WINDOW
                                        for f in range(M):
                                            mm = product(pe, o[w * WINDOW:(w + 1) * WINDOW, f * 256:(f + 1) * 256], [
                                                ([x[:, c, f, a:a + WINDOW] for x in (q_h, q_l)],
                                                 [x[:, f, 2 * p + w, :, :].rearrange("p a b -> p (a b)") for x in (kexp_h, kexp_l)])])
                                    mm.then_inc(filled, 1)
                            elif stage == "turn":
                                for p in range(lo, hi):
                                    o, filled = group((stage, c, p), ("prob_out", t, p))
                                    for h in range(4):
                                        mm = pe.transpose(o[:, h * P:(h + 1) * P],
                                                          prob[:, c, p, 2 * h:2 * h + 2, :].rearrange("p a b -> p (a b)"), idf[:, :])
                                    mm.then_inc(filled, 1)
                            elif stage == "mix":
                                for p in range(lo, hi):
                                    o, filled = group((stage, c, p), ("turn_out", t, p))
                                    for h in range(4):
                                        for w in range(2):
                                            r = (h % 2) * 2 * HD
                                            a = (h // 2) * P + w * WINDOW
                                            mm = product(pe, o[r:r + 2 * HD, a:a + WINDOW], [
                                                ([x[:, c, (2 * p + w) * 4 + h, :] for x in (vexp_h, vexp_l)],
                                                 [x[:, p, h, w * WINDOW:(w + 1) * WINDOW] for x in (pt_h, pt_l)])])
                                    mm.then_inc(filled, 1)
                            elif stage == "proj":
                                linear(stage, c, lo, hi, ("mix_lo", t, PAIRS - 1), "proj", M, D, *xs)

                    def settle():
                        pe.wait_ge(S["up0_out"], at("up0_out", 0, MH - 1))
                        pe.wait_ge(S["var_out"], at("var_out", 1))

                    run_parts(pe, steps, stages, settle)

                @block.scalar
                def _(act):
                    act.wait_ge(consts_made, 13)

                    def stages(i, part):
                        def keep(key):
                            r, _, _, before = plan_full[part][key]
                            if before is not None:
                                name, n = full_signal(before[0], before[2])
                                act.wait_ge(S[name], at(name, CH * (i + before[3]) + before[1], n))
                            return full[:, r, :]

                        for stage, c, lo, hi, ahead in parts_of(TOKENIZER)[part]:
                            t = CH * (i + ahead) + c
                            if stage == "conv":
                                act.wait_ge(tokens_stored[c], 16 * (i + ahead) + 16)
                                for m in range(lo, hi):
                                    o = product_of(act, i, part, (stage, c, m))
                                    act.activation(z[:, c, m, :], o[:, 0:N], ACT.Identity, bias=bias(col, "conv", m), scale=INV)
                                    act.activation(res[:, c, m, :], o[:, 0:N], ACT.Square, bias=bias(col, "conv", m),
                                                   scale=INV).then_inc(S["conv_out"], 1)
                            elif stage == "patches":
                                if part != "first" or c > 0:
                                    patches_high(act, i + ahead, c)
                            elif stage == "var":
                                o = product_of(act, i, part, (stage, c, 0))
                                act.activation(dev[:, c, :], o[:, 0:PAIRS], ACT.Sqrt, bias=epsc[:, 0:1]).then_inc(S["var_out"], 1)
                            elif stage in ("up0", "up1"):
                                for m in range(lo, hi):
                                    f = keep((stage, c, m))
                                    o = product_of(act, i, part, (stage, c, m))
                                    act.activation(f, o[:, 0:N], ACT.Gelu_apprx_tanh, bias=bias(col, "ff1", m),
                                                   scale=INV).then_inc(S[stage + "_out"], 1)
                            elif stage in ("down0", "down1", "proj"):
                                for m in range(lo, hi):
                                    f = keep((stage, c, m))
                                    o = product_of(act, i, part, (stage, c, m))
                                    act.activation(f, o[:, 0:N], ACT.Identity, bias=bias(col, "proj" if stage == "proj" else "ff2", m),
                                                   scale=INV).then_inc(S[stage + "_out"], 1)
                            elif stage == "query_key":
                                for n in range(lo, hi):
                                    f = keep((stage, c, n))
                                    o = product_of(act, i, part, (stage, c, n))
                                    a = act.activation(f, o[:, 0:N], ACT.Identity, bias=bias(col, "qkv", n), scale=INV)
                                    if n >= M:
                                        for h in range(4):
                                            r, e = h * HD, h * HD + HD
                                            a = act.activation(kexp_h[r:e, n - M, :, h, :],
                                                               o[r:e, 0:N].rearrange("p (w k) -> p w k", k=WINDOW),
                                                               ACT.Identity, bias=bias(col, "qkv", n, r, e), scale=INV)
                                    a.then_inc(S["query_key_out"], 1)
                            elif stage == "value":
                                for n in range(lo, hi):
                                    o = product_of(act, i, part, (stage, c, n))
                                    for r in range(2):
                                        a = act.activation(
                                            vexp_h[r * 64:r * 64 + 64, c, n * VROWS:n * VROWS + VROWS, r * HD:r * HD + HD],
                                            o[r * 64:r * 64 + 64, 0:VROWS * HD].rearrange("p (g x) -> p g x", x=HD),
                                            ACT.Copy)
                                    a.then_inc(S["v_hi"], 1)
                            elif stage == "score":
                                for p in range(lo, hi):
                                    act.wait_ge(S["score_out"], at("score_out", t, p))
                                    act.activation(prob[:, c, p, :, :], prob[:, c, p, :, :], ACT.Exp,
                                                   scale=HD ** -0.5).then_inc(S["prob_exp"], 1)
                            elif stage == "turn":
                                for p in range(lo, hi):
                                    o = product_of(act, i, part, (stage, c, p))
                                    act.activation(pt_h[:, p, :, :].rearrange("p a b -> p (a b)"), o[:, :], ACT.Copy).then_inc(S["turn_hi"], 1)
                            elif stage == "mix":
                                for p in range(lo, hi):
                                    f = keep((stage, c, p))
                                    o = product_of(act, i, part, (stage, c, p))
                                    for m in range(M):
                                        a = act.activation(f[:, m * P:m * P + P], o[:, m * P:m * P + P], ACT.Identity,
                                                           bias=bias(col, "qkv", 2 * M + m), scale=INV * INV)
                                    a.then_inc(S["mix_out"], 1)

                    def settle():
                        act.wait_ge(S["up0_lo"], at("up0_lo", 0, MH // 2 - 1))
                        act.wait_ge(S["up0_lo_odd"], at("up0_lo_odd", 0, MH // 2 - 1))

                    run_parts(act, steps, stages, settle)

                @block.vector
                def _(dve):
                    def stages(i, part):
                        def kept(key):
                            return full[:, plan_full[part][key][0], :]

                        def split(src, hi, lo, hi_name, lo_name, t, n=0):
                            dve.tensor_copy(hi, src).then_inc(S[hi_name], 1)
                            dve.wait_ge(S[hi_name], at(hi_name, t, n))
                            dve.tensor_tensor(lo, src, hi, ALU.subtract).then_inc(S[lo_name], 1)

                        for stage, c, lo, hi, ahead in parts_of(TOKENIZER)[part]:
                            t = CH * (i + ahead) + c
                            zc, rc = (x[:, c, :, :] for x in (z, res))
                            if stage == "var":
                                dve.wait_ge(S["var_out"], at("var_out", t))
                                dve.reciprocal(dev[:, c, :], dev[:, c, :]).then_inc(S["inverse"], 1)
                            elif stage == "rstd":
                                o = product_of(dve, i, part, (stage, c, 0))
                                dve.tensor_tensor(zc, zc, o[:, 0:N].unsqueeze(1).broadcast_to([P, M, N]),
                                                  ALU.mult).then_inc(S["rstd_out"], 1)
                                dve.wait_ge(S["table_biased"], at("table_biased", t, M - 1))
                                dve.wait_ge(S["rstd_out"], at("rstd_out", t))
                                for m in range(M):
                                    dve.scalar_tensor_tensor(rc[:, m, :], zc[:, m, :], bias(col, "ln_w", m), table[:, c, m * N:m * N + N],
                                                             ALU.mult, ALU.add).then_inc(S["residual"], 1)
                                dve.wait_ge(S["residual"], at("residual", t, M - 1))
                                split(rc, x_h[:, c, :, :], x_l[:, c, :, :], "x0_hi", "x0_lo", t)
                            elif stage in ("up0", "up1"):
                                for m in range(lo, hi):
                                    dve.wait_ge(S[stage + "_out"], at(stage + "_out", t, m))
                                    f, hi_part = kept((stage, c, m)), hid_h[:, c, m, :]
                                    dve.tensor_copy(hi_part, f).then_inc(S[stage + "_hi"], 1)
                                    if m % 2 == 0:
                                        dve.wait_ge(S[stage + "_hi"], at(stage + "_hi", t, m))
                                        dve.tensor_tensor(hid_l[:, c, m, :], f, hi_part, ALU.subtract).then_inc(S[stage + "_lo"], 1)
                            elif stage == "down0":
                                for m in range(lo, hi):
                                    dve.wait_ge(S["down0_out"], at("down0_out", t, m))
                                    split(kept((stage, c, m)), x_h[:, c, m, :], x_l[:, c, m, :], "down0_hi", "down0_lo", t, m)
                            elif stage == "query_key":
                                for n in range(lo, hi):
                                    dve.wait_ge(S["query_key_out"], at("query_key_out", t, n))
                                    f = kept((stage, c, n))
                                    if n < M:
                                        split(f, q_h[:, c, n, :], q_l[:, c, n, :], "q_hi", "q_lo", t, n)
                                        continue
                                    for h in range(4):
                                        r, e = h * HD, h * HD + HD
                                        d = dve.tensor_tensor(kexp_l[r:e, n - M, :, h, :],
                                                              f[r:e, :].rearrange("p (w k) -> p w k", k=WINDOW),
                                                              kexp_h[r:e, n - M, :, h, :], ALU.subtract)
                                    d.then_inc(S["k_lo"], 1)
                            elif stage == "value":
                                for n in range(lo, hi):
                                    dve.wait_ge(S["v_hi"], at("v_hi", t, n))
                                    b = plan_a[part][stage, c, n][0]
                                    for r in range(2):
                                        to = [x[r * 64:r * 64 + 64, c, n * VROWS:n * VROWS + VROWS, r * HD:r * HD + HD] for x in (vexp_h, vexp_l)]
                                        d = dve.tensor_tensor(
                                            to[1], bank[b][r * 64:r * 64 + 64, 0:VROWS * HD].rearrange("p (g x) -> p g x", x=HD),
                                            to[0], ALU.subtract)
                                    d.then_inc(S["value_out"], 1)
                            elif stage == "score":
                                for p in range(lo, hi):
                                    o = product_of(dve, i, part, (stage, c, p)).rearrange("p (h k) -> p h k", h=HEADS)
                                    dve.tensor_reduce(top[:, c, p, :], o, AX_X, ALU.max).then_inc(S["score_top"], 1)
                                    dve.wait_ge(S["score_top"], at("score_top", t, p))
                                    dve.tensor_tensor(prob[:, c, p, :, :], o, top[:, c, p, :].unsqueeze(2).broadcast_to([P, HEADS, WINDOW]),
                                                      ALU.subtract).then_inc(S["score_out"], 1)
                                for p in range(lo, hi):
                                    pr, rr = prob[:, c, p, :, :], rec[:, c, p, :]
                                    dve.wait_ge(S["prob_exp"], at("prob_exp", t, p))
                                    dve.tensor_reduce(rr, pr, AX_X, ALU.add).then_inc(S["prob_sum"], 1)
                                    dve.wait_ge(S["prob_sum"], at("prob_sum", t, p))
                                    dve.reciprocal(rr, rr).then_inc(S["prob_rec"], 1)
                                    dve.wait_ge(S["prob_rec"], at("prob_rec", t, p))
                                    dve.scalar_tensor_tensor(pr, pr, WS, rr.unsqueeze(2).broadcast_to([P, HEADS, WINDOW]),
                                                             ALU.mult, ALU.mult).then_inc(S["prob_out"], 1)
                            elif stage == "turn":
                                for p in range(lo, hi):
                                    dve.wait_ge(S["turn_hi"], at("turn_hi", t, p))
                                    b = plan_a[part][stage, c, p][0]
                                    hi, lo = (x[:, p, :, :].rearrange("p a b -> p (a b)") for x in (pt_h, pt_l))
                                    dve.tensor_tensor(lo, bank[b][:, :], hi, ALU.subtract).then_inc(S["turn_out"], 1)
                            elif stage == "mix":
                                for p in range(lo, hi):
                                    dve.wait_ge(S["mix_out"], at("mix_out", t, p))
                                    split(kept((stage, c, p))[:, 0:M * P].rearrange("p (m n) -> p m n", m=M),
                                          x_h[:, c, :, p * P:p * P + P], x_l[:, c, :, p * P:p * P + P], "mix_hi", "mix_lo", t, p)
                            elif stage == "proj":
                                for m in range(lo, hi):
                                    dve.wait_ge(S["proj_out"], at("proj_out", t, m))
                                    dve.tensor_tensor(res[:, c, m, :], kept((stage, c, m)), res[:, c, m, :], ALU.add).then_inc(S["attended"], 1)
                                    dve.wait_ge(S["attended"], at("attended", t, m))
                                    if m == 0:
                                        product_of(dve, i, part, (stage, c, M - 1))
                                    split(res[:, c, m, :], x_h[:, c, m, :], x_l[:, c, m, :], "x1_hi", "x1_lo", t, m)

                    run_parts(dve, steps, stages)

        with ExitStack() as ctx:
            hin = sb(ctx, "hin", [P, M, SEQ])
            z = sb(ctx, "lz", [P, M, SEQ])
            sq = sb(ctx, "lsq", [P, M, SEQ])
            dev = sb(ctx, "ldev", [P, CH, TILES])
            x_h = sb(ctx, "lx_h", [P, M, SEQ], F16)
            x_l = sb(ctx, "lx_l", [P, M, SEQ], F16)
            hin_h, hin_l, res_h, res_l = (sb(ctx, n, [P, M, SEQ], F16) for n in ("hin_h", "hin_l", "lres_h", "lres_l"))
            ones_h = sb(ctx, "ones_h", [P, P], F16)
            unit = sb(ctx, "unit", [P, 1])
            n_h = sb(ctx, "ln_h", [P, M, SEQ], F16)
            n_l = sb(ctx, "ln_l", [P, M, SEQ], F16)
            s_h = sb(ctx, "ls_h", [P, M, SEQ], F16)
            s_l = sb(ctx, "ls_l", [P, M, SEQ], F16)
            forget = sb(ctx, "forget", [P, M, SEQ])
            take = sb(ctx, "take", [P, M, SEQ])
            soft = sb(ctx, "soft", [P, M, SEQ])
            cand = sb(ctx, "cand", [P, M, SEQ])
            state = sb(ctx, "state", [P, 2, M, SEQ])
            res = sb(ctx, "lres", [P, M, SEQ])
            rh = sb(ctx, "rh", [P, SEQ])
            shape = [P, CH, TILES, EXPERTS]
            logit, mask1, mask2 = (sb(ctx, n, shape) for n in ("logit", "mask1", "mask2"))
            lim, rsum, gap, first_w, second_w = (sb(ctx, n, [P, CH, TILES]) for n in ("lim", "rsum", "gap", "first_w", "second_w"))
            chance = sb(ctx, "chance", [P, CH, TILES, 8])
            best = sb(ctx, "best", [P, CH, TILES, 8])
            best_at = sb(ctx, "best_at", [P, CH, TILES, 8], U32)
            best_f = sb(ctx, "best_f", [P, CH, TILES, 8])
            spare = sb(ctx, "spare", [P, 1])
            number = sb(ctx, "number", [P, TILES, EXPERTS])
            parts = sb(ctx, "parts", [P, CH, TILES, 2 * EXPERTS], F16)
            wt = sb(ctx, "wt", [2 * EXPERTS, SEQ + 3], F16)
            share = sb(ctx, "share", [P, EXPERTS, SEQ])
            full1 = sb(ctx, "full1", [P, 2, HALF[0]])
            full2 = sb(ctx, "full2", [P, 2, HALF[0]])
            h1_h = sb(ctx, "h1_h", [P, RING1, M, HALF[0]], F16)
            h1_l = sb(ctx, "h1_l", [P, RING1, M, HALF[0]], F16)
            h2_h = sb(ctx, "h2_h", [P, RING2, M, HALF[0]], F16)
            h2_l = sb(ctx, "h2_l", [P, RING2, M, HALF[0]], F16)
            ob = sb(ctx, "ob", [P, M, SEQ])
            layer_consts = sem("layer_consts")
            block = ctx.enter_context(nc.Block())

            sums = [bank[6], bank[7]]

            def at(name, t, n=0):
                return count(LAYER_SIGNALS, name, t, n)

            def product_of(eng, i, part, key):
                b, k, step, _ = plan_b[part][key]
                eng.wait_ge(bank_full[b], i * step + k + 1)
                return bank[b]

            def cut(c):
                return slice(START[c], START[c] + HALF[c])

            @block.sync
            def _(sp):
                first = [1, START[1]]
                size = [HALF[0] - 1, HALF[1]]
                for c in range(CH):
                    a = first[c]
                    sp.dma_start(hin[:, :, a:a + size[c]], tok[:, :, a - 1:a - 1 + size[c]]).then_inc(half_loaded[c], 16)

                def store(i, c):
                    sp.wait_ge(L["combined"], at("combined", CH * i + c, M - 1))
                    sp.dma_start(out[:, :, bass.ds(i * SEQ + START[c], HALF[c])], ob[:, :, cut(c)]).then_inc(out_stored[c], 16)

                def load(i, c):
                    sp.wait_ge(L["mixed"], at("mixed", CH * i + c))
                    a = first[c]
                    sp.dma_start(hin[:, :, a:a + size[c]], tok[:, :, bass.ds((i + 1) * PATCHES + a - 1, size[c])]
                                 ).then_inc(half_loaded[c], 16)

                load(0, 0)
                with sp.Fori(0, images - 2) as i:
                    load(i, 1)
                    store(i, 0)
                    load(i + 1, 0)
                    store(i, 1)
                load(images - 2, 1)
                for i in (images - 2, images - 1):
                    for c in range(CH):
                        store(i, c)
                for c in range(CH):
                    sp.wait_ge(out_stored[c], 16 * images + 16)

            @block.gpsimd
            def _(pool):
                pool.memset(chance[:], -1.0).then_inc(layer_consts, 1)
                for e in range(EXPERTS):
                    pool.memset(number[:, :, e:e + 1], float(e)).then_inc(layer_consts, 1)

                pool.memset(ones_h[:], 1.0 / D).then_inc(layer_consts, 1)
                pool.memset(unit[:], 1.0).then_inc(layer_consts, 1)
                pool.wait_ge(layer_consts, 4 + EXPERTS)

                def stages(i, part):
                    for stage, c, lo, hi, ahead in parts_of(LAYER)[part]:
                        t = CH * (i + ahead) + c
                        w = HALF[c]
                        if stage == "tokens":
                            pool.wait_ge(half_loaded[c], 16 * (i + ahead) + 16)
                            pool.wait_ge(L["mean1_out"], at("mean1_out", t - CH))
                            to = [x[:, :, cut(c)] for x in (hin_h, hin_l)]
                            pool.tensor_tensor(to[0], hin[:, :, cut(c)], unit[:, 0:1].unsqueeze(2).broadcast_to([P, M, w]),
                                               ALU.mult).then_inc(L["token_hi"], 1)
                            pool.wait_ge(L["token_hi"], at("token_hi", t))
                            pool.tensor_tensor(to[1], hin[:, :, cut(c)], to[0], ALU.subtract).then_inc(L["token_lo"], 1)
                        elif stage in ("mean1", "mean2"):
                            k = stage[-1]
                            pool.wait_ge(L["squared" + k], at("squared" + k, t))
                            pool.tensor_tensor(sq[:, 0, cut(c)], sq[:, 0, cut(c)], sq[:, 1, cut(c)], ALU.add
                                               ).then_inc(L["summed" + k], 1)
                        elif stage == "expert2":
                            for n in range(lo, hi):
                                if n == 0:
                                    pool.wait_ge(L["share_out"], at("share_out", t, EXPERTS - 1))
                                pool.wait_ge(L["expert2_out"], at("expert2_out", t, n))
                                pool.tensor_tensor(full2[:, n % M, 0:w], full2[:, n % M, 0:w], share[:, n // M, cut(c)],
                                                   ALU.mult).then_inc(L["h2_weighted"], 1)

                run_parts(pool, images, stages)

            @block.tensor
            def _(pe):
                pe.wait_ge(layer_consts, 4 + EXPERTS)
                def stages(i, part):
                    def group(key, ready=None):
                        b, _, _, before = plan_b[part][key]
                        s = None if before is None else before[0]
                        if ready is not None:
                            pe.wait_ge(L[ready[0]], at(*ready))
                        if s is not None and (ready is None or ready[0] != s + "_out"):
                            pe.wait_ge(L[s + "_out"], at(s + "_out", CH * (i + before[3]) + before[1], before[2]))
                        return bank[b], bank_full[b]

                    for stage, c, lo, hi, ahead in parts_of(LAYER)[part]:
                        t = CH * (i + ahead) + c
                        w = HALF[c]
                        if stage[:-1] in ("mean", "var"):
                            ready = {"mean1": "token_lo", "mean2": "mixed_lo", "var1": "summed1", "var2": "summed2"}[stage], t
                            o, filled = group((stage, c, 0), ready)
                            if stage[:-1] == "mean":
                                terms = [x[:, m, cut(c)] for x in ((hin_h, hin_l) if stage == "mean1" else (res_h, res_l))
                                         for m in range(M)]
                                for k, x in enumerate(terms):
                                    mm = pe.matmul(o[:, 0:w], ones_h[:, :], x, start=(k == 0), stop=(k == len(terms) - 1))
                                mm.then_inc(filled, 1)
                                continue
                            for j in range(TILES):
                                a = START[c] + j * TSTEP
                                mm = pe.matmul(o[0:TILE[c], j:j + 1], sq[:, 0, a:a + TILE[c]], ones[:, 0:1], start=True, stop=True)
                            mm.then_inc(filled, 1)
                        elif stage[:-1] == "rstd":
                            o, filled = group((stage, c, 0), ("inverse" + stage[-1], t))
                            q = TILE[c]
                            for j in range(TILES):
                                mm = pe.matmul(o[:, j * TSTEP:j * TSTEP + q], dev[0:q, c, j:j + 1].broadcast_to([q, P]), idf[0:q, 0:q],
                                               start=True, stop=True)
                            mm.then_inc(filled, 1)
                        elif stage in ("gru0", "gru1"):
                            name = "norm1_lo" if stage == "gru0" else "state0_lo"
                            xs = (n_h, n_l) if stage == "gru0" else (s_h, s_l)
                            for n in range(lo, hi):
                                o, filled = group((stage, c, n), (name, t) if n == lo else None)
                                f = (n % 2) * M + n // 2
                                product(pe, o[:, 0:w], [
                                    ([weight(x, WB[stage], k, 2 * D, f * P, f * P + P) for x in (wbh, wbl)],
                                     [x[:, k, cut(c)] for x in xs]) for k in range(M)]).then_inc(filled, 1)
                        elif stage == "router1":
                            o, filled = group(("router1", c, 0), ("norm2_lo", t))
                            product(pe, o[:, 0:w], [
                                ([weight(x, WB["router1"], k, ROUTER, 0, ROUTER) for x in (wbh, wbl)],
                                 [x[:, k, cut(c)] for x in (x_h, x_l)]) for k in range(M)]).then_inc(filled, 1)
                        elif stage == "router2":
                            o, filled = group(("router2", c, 0), ("router1_out", t))
                            for j in range(TILES):
                                a = START[c] + j * TSTEP
                                mm = pe.matmul(o[0:TILE[c], j * EXPERTS:(j + 1) * EXPERTS], rh[:, a:a + TILE[c]],
                                               col[:, BC["router2_w"]:BC["router2_w"] + EXPERTS], start=True, stop=True)
                            mm.then_inc(filled, 1)
                        elif stage == "weights":
                            o, filled = group(("weights", c, 0), ("route", t, ROUTE_STEPS - 1))
                            for j in range(TILES):
                                a = j * TSTEP
                                mm = pe.transpose(o[0:2 * EXPERTS, :].bitcast(F16)[:, a:a + TILE[c]],
                                                  parts[0:TILE[c], c, j, :], idh[0:TILE[c], 0:TILE[c]])
                            mm.then_inc(filled, 1)
                        elif stage == "share":
                            for e in range(EXPERTS):
                                o, filled = group((stage, c, e), ("weights_out", t) if e == 0 else None)
                                pe.matmul(o[:, 0:w], sel[:, e * P:e * P + P], wt[:, cut(c)], start=True, stop=True).then_inc(filled, 1)
                        elif stage[:-1] == "expert":
                            layer, e = int(stage[-1]), lo // M
                            if layer == 1:
                                ready = None
                                xs = [[x[:, k, cut(c)] for x in (x_h, x_l)] for k in range(M)]
                            elif layer == 2:
                                ready = ("h1_lo", t, e * M + M - 1)
                                xs = [[x[:, e % RING1, k, 0:w] for x in (h1_h, h1_l)] for k in range(M)]
                            else:
                                pe.wait_ge(L["h2_lo"], at("h2_lo", t, e * M + M - 1))
                                xs = [[x[:, e % RING2, k, 0:w] for x in (h2_h, h2_l)] for k in range(M)]
                                if e == 0:
                                    pe.wait_ge(L["combined"], at("combined", t - 1, M - 1))
                            for m in range(M):
                                ws = [[weight(x, WB["expert%d" % layer] + e * M * D, k, D, m * P, m * P + P) for x in (wbh, wbl)]
                                      for k in range(M)]
                                if layer < 3:
                                    o, filled = group((stage, c, e * M + m), ready if m == 0 else None)
                                    product(pe, o[:, 0:w], list(zip(ws, xs))).then_inc(filled, 1)
                                    continue
                                for k in range(M):
                                    for n, (a, b) in enumerate(((0, 0), (0, 1), (1, 0))):
                                        pe.matmul(sums[m][:, 0:w], ws[k][a], xs[k][b],
                                                  start=(e == 0 and k == 0 and n == 0), stop=False)
                                if e == EXPERTS - 1:
                                    pe.matmul(sums[m][:, 0:w], b3h[:, m * P:m * P + P], wt[:, cut(c)], start=False, stop=False)
                                    pe.matmul(sums[m][:, 0:w], b3l[:, m * P:m * P + P], wt[:, cut(c)],
                                              start=False, stop=True).then_inc(L["sums_full"], 1)

                def settle():
                    pe.wait_ge(L["share_out"], at("share_out", 0, EXPERTS - 1))
                    pe.wait_ge(L["gru1_out"], at("gru1_out", 1, 2 * M - 1))

                run_parts(pe, images, stages, settle)

            @block.scalar
            def _(act):
                def stages(i, part):
                    for stage, c, lo, hi, ahead in parts_of(LAYER)[part]:
                        t = CH * (i + ahead) + c
                        w = HALF[c]
                        if stage[:-1] == "mean":
                            k = stage[-1]
                            act.wait_ge(L[stage + "_out"], at(stage + "_out", t))
                            act.activation(sq[:, :, cut(c)], z[:, :, cut(c)], ACT.Square).then_inc(L["squared" + k], 1)
                        elif stage[:-1] == "var":
                            o = product_of(act, i, part, (stage, c, 0))
                            act.activation(dev[0:TILE[c], c, :], o[0:TILE[c], 0:TILES], ACT.Sqrt, bias=epsc[0:TILE[c], 0:1]
                                           ).then_inc(L[stage + "_out"], 1)
                        elif stage in ("gru0", "gru1"):
                            for n in range(lo, hi):
                                o, m, f = product_of(act, i, part, (stage, c, n)), n // 2, (n % 2) * M + n // 2
                                if n % 2 == 0:
                                    act.activation(forget[:, m, cut(c)], o[:, 0:w], ACT.Sigmoid, bias=bias(ncol, stage, f), scale=-INV)
                                    act.activation(take[:, m, cut(c)], o[:, 0:w], ACT.Sigmoid, bias=bias(col, stage, f),
                                                   scale=INV).then_inc(L[stage + "_out"], 1)
                                else:
                                    act.activation(soft[:, m, cut(c)], o[:, 0:w], ACT.Sigmoid, bias=bias(col, stage, f), scale=INV)
                                    act.activation(cand[:, m, cut(c)], o[:, 0:w], ACT.Relu, bias=bias(col, stage, f),
                                                   scale=INV).then_inc(L[stage + "_out"], 1)
                        elif stage == "router1":
                            o = product_of(act, i, part, ("router1", c, 0))
                            act.activation(rh[:, cut(c)], o[:, 0:w], ACT.Relu, bias=bias(col, "router1", 0),
                                           scale=INV).then_inc(L["router1_out"], 1)
                        elif stage == "router2":
                            lg = logit[0:TILE[c], c, :, :].rearrange("p a b -> p (a b)")
                            act.wait_ge(L["route"], at("route", t, 1))
                            act.activation(lg, lg, ACT.Exp).then_inc(L["router_exp"], 1)
                            act.wait_ge(L["route"], at("route", t, 8))
                            act.activation(gap[0:TILE[c], c, :], gap[0:TILE[c], c, :], ACT.Exp).then_inc(L["router_exp2"], 1)
                        elif stage == "share":
                            for e in range(EXPERTS):
                                o = product_of(act, i, part, (stage, c, e))
                                act.activation(share[:, e, cut(c)], o[:, 0:w], ACT.Copy).then_inc(L["share_out"], 1)
                        elif stage == "expert1":
                            for n in range(lo, hi):
                                e, m = n // M, n % M
                                act.wait_ge(L["h1_lo"], at("h1_lo", t, n - 2))
                                o = product_of(act, i, part, (stage, c, n))
                                for to in (h1_h[:, e % RING1, m, 0:w], full1[:, m, 0:w]):
                                    a = act.activation(to, o[:, 0:w], ACT.Relu, bias=bias(col, stage, n), scale=INV)
                                a.then_inc(L["expert1_out"], 1)
                        elif stage == "expert2":
                            used, ring = "h2_lo", full2
                            for n in range(lo, hi):
                                act.wait_ge(L[used], at(used, t, n - 2))
                                o = product_of(act, i, part, (stage, c, n))
                                act.activation(ring[:, n % M, 0:w], o[:, 0:w], ACT.Relu, bias=bias(col, stage, n),
                                               scale=INV).then_inc(L[stage + "_out"], 1)

                run_parts(act, images, stages)

            @block.vector
            def _(dve):
                dve.tensor_copy(hin[:, :, 0:1], col[:, BC["cls"]:BC["cls"] + M].unsqueeze(2)).then_inc(layer_consts, 1)
                dve.wait_ge(layer_consts, 4 + EXPERTS)
                def stages(i, part):
                    def split(src, hi, lo, hi_name, lo_name, t, n=0):
                        dve.tensor_copy(hi, src).then_inc(L[hi_name], 1)
                        dve.wait_ge(L[hi_name], at(hi_name, t, n))
                        dve.tensor_tensor(lo, src, hi, ALU.subtract).then_inc(L[lo_name], 1)

                    for stage, c, lo, hi, ahead in parts_of(LAYER)[part]:
                        t = CH * (i + ahead) + c
                        w = HALF[c]
                        zc = z[:, :, cut(c)]
                        if stage[:-1] == "mean":
                            o = product_of(dve, i, part, (stage, c, 0))
                            src = hin if stage == "mean1" else res
                            dve.tensor_tensor(zc, src[:, :, cut(c)], o[:, 0:w].unsqueeze(1).broadcast_to([P, M, w]),
                                              ALU.subtract).then_inc(L[stage + "_out"], 1)
                        elif stage[:-1] == "var":
                            k = stage[-1]
                            dve.wait_ge(L[stage + "_out"], at(stage + "_out", t))
                            dve.reciprocal(dev[0:TILE[c], c, :], dev[0:TILE[c], c, :]).then_inc(L["inverse" + k], 1)
                        elif stage[:-1] == "rstd":
                            k = stage[-1]
                            o = product_of(dve, i, part, (stage, c, 0))
                            dve.tensor_tensor(zc, zc, o[:, 0:w].unsqueeze(1).broadcast_to([P, M, w]),
                                              ALU.mult).then_inc(L[stage + "_out"], 1)
                            dve.wait_ge(L[stage + "_out"], at(stage + "_out", t))
                            hi, lo = (n_h, n_l) if k == "1" else (x_h, x_l)
                            split(zc, hi[:, :, cut(c)], lo[:, :, cut(c)], "norm%s_hi" % k, "norm%s_lo" % k, t)
                        elif stage in ("gru0", "gru1"):
                            g = int(stage[-1])
                            for m in range(lo // 2, hi // 2):
                                ca, so, ta, fo = (x[:, m, cut(c)] for x in (cand, soft, take, forget))
                                dve.wait_ge(L[stage + "_out"], at(stage + "_out", t, 2 * m + 1))
                                dve.scalar_tensor_tensor(ca, so, 0.5, ca, ALU.min, ALU.add).then_inc(L["candidate%d" % g], 1)
                                dve.wait_ge(L["candidate%d" % g], at("candidate%d" % g, t, m))
                                dve.tensor_tensor(ca, ca, ta, ALU.mult).then_inc(L["taken%d" % g], 1)
                                dve.wait_ge(L["taken%d" % g], at("taken%d" % g, t, m))
                                if c == 0:
                                    before = 0.5
                                else:
                                    dve.wait_ge(L["state%d" % g], at("state%d" % g, t - 1, m))
                                    before = state[:, g, m, START[c] - 1:START[c]]
                                dve.tensor_tensor_scan(state[:, g, m, cut(c)], fo, ca, before, ALU.mult, ALU.add
                                                       ).then_inc(L["state%d" % g], 1)
                            if g == 0 and hi == 2 * M:
                                dve.wait_ge(L["state0"], at("state0", t, M - 1))
                                split(state[:, 0, :, cut(c)], s_h[:, :, cut(c)], s_l[:, :, cut(c)], "state0_hi", "state0_lo", t)
                        elif stage == "mixed":
                            dve.wait_ge(L["combined"], at("combined", t - CH, M - 1))
                            dve.wait_ge(L["state1"], at("state1", t, M - 1))
                            dve.tensor_tensor(res[:, :, cut(c)], state[:, 1, :, cut(c)], hin[:, :, cut(c)],
                                              ALU.add).then_inc(L["mixed"], 1)
                            dve.wait_ge(L["mixed"], at("mixed", t))
                            split(res[:, :, cut(c)], res_h[:, :, cut(c)], res_l[:, :, cut(c)], "mixed_hi", "mixed_lo", t)
                        elif stage == "router2":
                            q = TILE[c]
                            done = [0]

                            def step(d):
                                d.then_inc(L["route"], 1)
                                dve.wait_ge(L["route"], at("route", t, done[0]))
                                done[0] += 1

                            def wide(x):
                                return x.unsqueeze(2).broadcast_to([q, TILES, EXPERTS])

                            lg, m1, m2 = (x[0:q, c, :, :] for x in (logit, mask1, mask2))
                            lm, rs, gp, fw, sw = (x[0:q, c, :] for x in (lim, rsum, gap, first_w, second_w))
                            ch = chance[0:q, c, :, :]
                            o = product_of(dve, i, part, ("router2", c, 0))[0:q, 0:TILES * EXPERTS].rearrange("p (a b) -> p a b", a=TILES)
                            b2 = col[0:q, BC["router2"]:BC["router2"] + EXPERTS].unsqueeze(1).broadcast_to([q, TILES, EXPERTS])
                            dve.tensor_tensor(lg, o, b2, ALU.add).then_inc(L["router2_out"], 1)
                            dve.wait_ge(L["router2_out"], at("router2_out", t))
                            step(dve.tensor_reduce(lm, lg, AX_X, ALU.max))
                            step(dve.tensor_tensor(lg, lg, wide(lm), ALU.subtract))
                            dve.wait_ge(L["router_exp"], at("router_exp", t))
                            step(dve.tensor_reduce(rs, lg, AX_X, ALU.add))
                            step(dve.reciprocal(rs, rs))
                            step(dve.tensor_tensor(ch[:, :, 0:EXPERTS], lg, wide(rs), ALU.mult))
                            dve.tensor_copy(spare[0:q, :], ch[:, 0, 0:1])
                            for j in range(TILES):
                                d = dve.max(best[0:q, c, j, :], ch[:, j, :])
                            step(d)
                            dve.tensor_copy(spare[0:q, :], best[0:q, c, 0, 0:1])
                            for j in range(TILES):
                                d = dve.max_index(best_at[0:q, c, j, :], best[0:q, c, j, :], ch[:, j, :])
                            step(d)
                            step(dve.tensor_copy(best_f[0:q, c, :, :], best_at[0:q, c, :, :]))
                            step(dve.tensor_tensor(gp, best[0:q, c, :, 1], best[0:q, c, :, 0], ALU.subtract))
                            num = number[0:q, :, :]
                            step(dve.tensor_tensor(m1, num, wide(best_f[0:q, c, :, 0]), ALU.is_equal))
                            step(dve.tensor_tensor(m2, num, wide(best_f[0:q, c, :, 1]), ALU.is_equal))
                            dve.wait_ge(L["router_exp2"], at("router_exp2", t))
                            step(dve.tensor_scalar(fw, gp, 1.0, None, ALU.add))
                            step(dve.reciprocal(fw, fw))
                            step(dve.tensor_tensor(sw, gp, fw, ALU.mult))
                            step(dve.tensor_tensor(m1, m1, wide(fw), ALU.mult))
                            step(dve.tensor_tensor(m2, m2, wide(sw), ALU.mult))
                            step(dve.tensor_tensor(m1, m1, m2, ALU.add))
                            pa = parts[0:q, c, :, :]
                            step(dve.tensor_copy(pa[:, :, 0:EXPERTS], m1))
                            step(dve.tensor_tensor(pa[:, :, EXPERTS:2 * EXPERTS], m1, pa[:, :, 0:EXPERTS], ALU.subtract))
                        elif stage == "weights":
                            o = product_of(dve, i, part, ("weights", c, 0))[0:2 * EXPERTS, :].bitcast(F16)[:, 0:w]
                            dve.tensor_copy(wt[:, cut(c)], o).then_inc(L["weights_out"], 1)
                        elif stage == "expert1":
                            for n in range(lo, hi):
                                e, m = n // M, n % M
                                dve.wait_ge(L["expert1_out"], at("expert1_out", t, n))
                                dve.tensor_tensor(h1_l[:, e % RING1, m, 0:w], full1[:, m, 0:w], h1_h[:, e % RING1, m, 0:w],
                                                  ALU.subtract).then_inc(L["h1_lo"], 1)
                        elif stage == "expert2":
                            for n in range(lo, hi):
                                e, m = n // M, n % M
                                dve.wait_ge(L["h2_weighted"], at("h2_weighted", t, n))
                                split(full2[:, m, 0:w], h2_h[:, e % RING2, m, 0:w], h2_l[:, e % RING2, m, 0:w], "h2_hi", "h2_lo", t, n)
                        elif stage == "expert3" and hi == EXPERTS * M:
                            dve.wait_ge(out_stored[c], 16 * i + 16)
                            for m in range(M):
                                dve.wait_ge(L["sums_full"], at("sums_full", t, m))
                                dve.scalar_tensor_tensor(ob[:, m, cut(c)], sums[m][:, 0:w], INV, res[:, m, cut(c)],
                                                         ALU.mult, ALU.add).then_inc(L["combined"], 1)

                run_parts(dve, images, stages)


def _by_input(w):
    k, n = w.shape
    return w.reshape(k // P, P, n).transpose(1, 0, 2).reshape(P, -1)


def _positions():
    place = np.arange(PATCHES, dtype=np.float32)[:, None]
    i = np.arange(0, D, 2, dtype=np.float32)
    angle = place * np.exp(-np.log(np.float32(10000.0)) * i / np.float32(D)).astype(np.float32)
    pe = np.stack([np.sin(angle), np.cos(angle)], axis=-1).reshape(PATCHES, D).astype(np.float32)
    every = np.tile(pe, (IMAGES, 1))
    return np.ascontiguousarray(every.reshape(TOKENS // N, N, M, P).transpose(0, 3, 2, 1).reshape(TOKENS // N, P, M * N))


def kernel(x, cls_tok, **w):
    import concourse.bacc as bacc
    from concourse.bass_utils import run_bass_kernel_spmd as run

    g = {k[3:]: np.asarray(v) for k, v in w.items()}
    side = SIDE // PATCH
    patches = np.asarray(x).reshape(IMAGES, CHANNELS, side, PATCH, side, PATCH).transpose(1, 3, 5, 0, 2, 4)
    patches = patches.reshape(KP, P, TOKENS // N, N).transpose(2, 1, 0, 3).reshape(TOKENS // N, P, KP * N)
    wa = np.concatenate([_by_input(g["tok_conv_w"].reshape(D, -1).T), _by_input(g["tok_ff_w1"].T), _by_input(g["tok_ff_w2"].T),
                         _by_input(g["tok_qkv_w"].T), _by_input(g["tok_proj_w"].T)], axis=1)
    wb = np.concatenate([_by_input(g["attn_W0"].T), _by_input(g["attn_W1"].T), _by_input(g["ffn_router_w1"])]
                        + [_by_input(g["ffn_expert_w%d" % k][e]) for k in (1, 2, 3) for e in range(EXPERTS)], axis=1)

    def tall(v):
        return v.reshape(-1, P).T

    rows = [tall(g["tok_" + n]) for n in ("conv_b", "ln_w", "ln_b", "ff_b1", "ff_b2", "qkv_b", "proj_b")]
    rows += [tall(g[n]) for n in ("attn_b0", "attn_b1", "ffn_router_b1", "ffn_expert_b1", "ffn_expert_b2")]
    rows += [np.tile(g["ffn_router_b2"], (P, 1)), g["ffn_router_w2"],
             tall(np.asarray(cls_tok))]
    b3 = np.zeros((2 * EXPERTS, D + EXPERTS * P), np.float32)
    b3[:EXPERTS, :D] = b3[EXPERTS:, :D] = g["ffn_expert_b3"]
    for e in range(EXPERTS):
        b3[[e, EXPERTS + e], D + e * P:D + e * P + P] = 1.0
    arrays = {
        "patches": patches, "positions": _positions(), "tokenizer_weights": wa, "layer_weights": wb,
        "columns": np.concatenate(rows, axis=1), "last_bias": b3,
        "identity": np.eye(P, dtype=np.float32),
    }
    arrays = {k: np.ascontiguousarray(v) for k, v in arrays.items()}
    nc = bacc.Bacc("TRN2", target_bir_lowering=False, num_devices=1)
    args = [nc.dram_tensor(k, a.shape, mybir.dt.from_np(a.dtype), kind="ExternalInput").ap() for k, a in arrays.items()]
    args.append(nc.dram_tensor("out", (P, M, IMAGES * SEQ), F32, kind="ExternalOutput").ap())
    build_program(nc, *args)
    r = run(nc, [arrays], core_ids=[0])
    return r.results[0]["out"].reshape(P, M, IMAGES, SEQ).transpose(2, 3, 1, 0).reshape(IMAGES, SEQ, D)
```
